# Optimizing a Trainium2 kernel written in Bass

```python
import numpy as np
import jax
import jax.numpy as jnp

def _softmax(x, axis=-1):
    return jax.nn.softmax(x, axis=axis)

def _gelu(x):
    return jax.nn.gelu(x, approximate=True)

def _silu(x):
    return jax.nn.silu(x)

def _sigmoid(x):
    return jax.nn.sigmoid(x)

def _layernorm(x, axis=-1, eps=1e-05):
    m = jnp.mean(x, axis=axis, keepdims=True)
    v = jnp.var(x, axis=axis, keepdims=True)
    return (x - m) / jnp.sqrt(v + eps)

def _scatter_add(tgt, idx, src, axis=0):
    return tgt.at[idx].add(src)

def _segment_sum(src, seg, n):
    return jax.ops.segment_sum(src, seg, n)
kernel_name = 'mk_xattn_seq_d1_seqx_r2_d48443'

def setup_inputs(seed: int=0):
    np.random.seed(seed)
    _w = jnp.asarray

    def _rec_inputs():
        import jax
        import jax.numpy as jnp
        _rk = jax.random.key(seed)
        x = -0.000125 + 0.9999 * jax.random.normal(jax.random.fold_in(_rk, 1), (16, 512, 512), jnp.float32)
        _lenS = 512 - jax.random.randint(jax.random.fold_in(_rk, 7), (16,), 0, max(1, 512 // 4) + 1, jnp.int32)
        _lenS2 = 120 - jax.random.randint(jax.random.fold_in(_rk, 8), (16,), 0, max(1, 120 // 4) + 1, jnp.int32)
        _ctx_512P = jax.random.normal(jax.random.fold_in(_rk, 11), (16, 16, 256), jnp.float32)
        _ctx_512c = jax.random.dirichlet(jax.random.fold_in(_rk, 511), 0.3 * jnp.ones((16,), jnp.float32), (16, 120))
        _ctx_512t = jnp.einsum('bsk,bkd->bsd', _ctx_512c, _ctx_512P)
        _ctx_512t = _ctx_512t * jax.lax.rsqrt(jnp.mean(jnp.square(_ctx_512t)) + 1e-12) * 0.953939
        ctx_512 = 0.000227908 + 0.99994 * (_ctx_512t + 0.3 * jax.random.normal(jax.random.fold_in(_rk, 611), (16, 120, 256), jnp.float32))
        return (x, ctx_512)
    x, ctx_512 = _rec_inputs()

    def _L0_xattn_setup():
        import jax, jax.numpy as jnp
        import numpy as np
        B, T, E = (8, 2048, 512)
        M, L = (128, 256)
        EPS = 1e-06
        key = jax.random.key(seed)
        ks = jax.random.split(key, 5)
        return {'emb': jax.random.normal(ks[0], (B, T, E), dtype=jnp.float32), 'latent': jax.random.normal(ks[1], (B, M, L), dtype=jnp.float32), 'Wq': jax.random.normal(ks[2], (E, E), dtype=jnp.float32) * (1.0 / np.sqrt(E)), 'bq': jnp.zeros((E,), dtype=jnp.float32), 'Wk': jax.random.normal(ks[3], (L, E), dtype=jnp.float32) * (1.0 / np.sqrt(L)), 'bk': jnp.zeros((E,), dtype=jnp.float32), 'Wv': jax.random.normal(ks[4], (L, E), dtype=jnp.float32) * (1.0 / np.sqrt(L)), 'bv': jnp.zeros((E,), dtype=jnp.float32), 'gamma': jnp.ones((E,), dtype=jnp.float32), 'beta': jnp.zeros((E,), dtype=jnp.float32)}
    _L0_xattn_all = _L0_xattn_setup()
    _L0_xattn_in = {k: v for k, v in _L0_xattn_all.items() if k in ('Wq', 'bq', 'Wk', 'bk', 'Wv', 'bv', 'gamma', 'beta')}
    del _L0_xattn_all
    return {'x': x, 'ctx_512': ctx_512, 'L0_xattn_Wq': _L0_xattn_in['Wq'], 'L0_xattn_bq': _L0_xattn_in['bq'], 'L0_xattn_Wk': _L0_xattn_in['Wk'], 'L0_xattn_bk': _L0_xattn_in['bk'], 'L0_xattn_Wv': _L0_xattn_in['Wv'], 'L0_xattn_bv': _L0_xattn_in['bv'], 'L0_xattn_gamma': _L0_xattn_in['gamma'], 'L0_xattn_beta': _L0_xattn_in['beta']}

def reference(x, ctx_512, L0_xattn_Wq, L0_xattn_bq, L0_xattn_Wk, L0_xattn_bk, L0_xattn_Wv, L0_xattn_bv, L0_xattn_gamma, L0_xattn_beta):
    import jax
    import jax.numpy as jnp

    def _L0_xattn_ref(emb, latent, Wq, bq, Wk, bk, Wv, bv, gamma, beta):
        import jax, jax.numpy as jnp
        import numpy as np
        B, T, E = (8, 2048, 512)
        M, L = (128, 256)
        EPS = 1e-06
        q = jnp.einsum('bte,ef->btf', emb, Wq) + bq
        k = jnp.einsum('bml,le->bme', latent, Wk) + bk
        v = jnp.einsum('bml,le->bme', latent, Wv) + bv
        scale = 1.0 / jnp.sqrt(jnp.asarray(E, dtype=q.dtype))
        w = jnp.einsum('bte,bme->btm', q, k) * scale
        w = jax.nn.softmax(w, axis=1)
        pred = jnp.einsum('btm,bme->bte', w, v)
        x = pred + emb
        mu = jnp.mean(x, axis=-1, keepdims=True)
        var = jnp.var(x, axis=-1, keepdims=True)
        return (x - mu) * jax.lax.rsqrt(var + EPS) * gamma + beta
    x = _L0_xattn_ref(x, ctx_512, L0_xattn_Wq, L0_xattn_bq, L0_xattn_Wk, L0_xattn_bk, L0_xattn_Wv, L0_xattn_bv, L0_xattn_gamma, L0_xattn_beta)
    return x

_drawn_inputs = setup_inputs


def setup_inputs(seed=0):
    import zlib

    import numpy as np

    out = dict(_drawn_inputs(seed))
    spreads = {'L0_xattn_bq': (0.0, 0.8),
     'L0_xattn_bk': (0.0, 0.572),
     'L0_xattn_bv': (0.0, 0.306),
     'L0_xattn_gamma': (1.0, 0.2),
     'L0_xattn_beta': (0.0, 0.1)}
    factors = {}
    for name, (base, spread) in spreads.items():
        noise = np.random.default_rng([zlib.crc32(name.encode()), seed]).standard_normal(out[name].shape)
        drawn = base * np.exp(spread * noise) if base else spread * noise
        out[name] = jnp.asarray(drawn.astype(out[name].dtype))
    for name, factor in factors.items():
        out[name] = (out[name] * factor).astype(out[name].dtype)
    return out
```

```python
from contextlib import ExitStack

import concourse.bass as bass
from concourse import mybir

P = 128
F32 = mybir.dt.float32
ALU = mybir.AluOpType
ACT = mybir.ActivationFunctionType
AX = mybir.AxisListType

EPS = 1e-6
RING = 4
LOOP_FROM = 2
POOL_J = 3


def cross_attention(nc, x, ctx_in, Wq, bq, Wk, bk, Wv, bv, gamma, beta, out):
    B, T, E = x.shape
    _, M, L = ctx_in.shape
    RJ = T // P
    EC = E // P
    FC = Wq.shape[1] // P
    LC = L // P
    LOOP_TO = LOOP_FROM + (B - 1 - LOOP_FROM) // RING * RING
    SCALE = float(E) ** -0.5
    assert T == RJ * P and E == EC * P and L == LC * P and M <= P and EC * M + 1 <= 512

    with ExitStack() as stack:
        def sb(name, shape, dt=F32):
            return stack.enter_context(nc.sbuf_tensor(name, shape, dt))

        def bank(name, shape, dt=F32):
            return stack.enter_context(nc.psum_tensor(name, shape, dt))

        def sem(name):
            return stack.enter_context(nc.semaphore(name))

        ident = sb("ident", [P, P])
        wq_nat = sb("wq_nat", [P, EC, E])
        wk_nat = sb("wk_nat", [P, LC, E])
        wqT = sb("wqT", [P, FC, E])
        wkT = sb("wkT", [P, FC, L])
        wv = sb("wv", [P, LC, E])
        qkT = sb("qkT", [P, LC, E])
        bq_all = sb("bq_all", [P, E])
        bk_all = sb("bk_all", [P, E])
        bv_all = sb("bv_all", [P, E])
        gamma_all = sb("gamma_all", [P, E])
        beta_all = sb("beta_all", [P, E])
        dot_junk = sb("dot_junk", [P, EC + LC + 1, E])
        u_col = sb("u_col", [P, EC])
        w_col = sb("w_col", [P, LC])
        d_col = sb("d_col", [P, 1])
        ctx_nat = sb("ctx_nat", [M, RING, L])
        ctxT = sb("ctxT", [P, 2, LC, M])
        xbuf = sb("xbuf", [P, RING, RJ, E])
        xT = sb("xT", [P, EC, T])
        gT = sb("gT", [P, EC, M])
        c_key = sb("c_key", [M, 2, 1])
        probs = sb("probs", [M, T])
        v_raw = sb("v_raw", [M, 2, E])
        v_soft = sb("v_soft", [M, E])
        s_max = sb("s_max", [M, 1])
        s_neg = sb("s_neg", [M, 1])
        s_bias = sb("s_bias", [M, 1])
        s_sum = sb("s_sum", [M, 1])
        s_rec = sb("s_rec", [M, 1])
        stats = sb("stats", [P, RJ, 6])
        mean_var = sb("mean_var", [P, RJ, 2])
        var_eps = sb("var_eps", [P, RJ])
        neg_mean = sb("neg_mean", [P, RJ])
        minus_half = sb("minus_half", [P, RJ])
        rstd = sb("rstd", [P, 2, RJ])
        shift = sb("shift", [P, RJ])

        xT_ps = [bank(f"xT_ps{i}", [P, RJ, P]) for i in range(2)]
        ctx_ps = bank("ctx_ps", [P, 512])
        v_ps = bank("v_ps", [P, 512])
        g_ps = bank("g_ps", [P, 512])
        s_ps = bank("s_ps", [P, 512])
        pv_ps = [bank(f"pv_ps{i}", [P, 512]) for i in range(2)]
        ctxT_v = ctx_ps[:, 0:LC * M].rearrange("p (c m) -> p c m", m=M)
        g_v = g_ps[:, 0:EC * M].rearrange("p (c m) -> p c m", m=M)
        ckey_v = g_ps[0:M, EC * M:EC * M + 1]

        ident_set = sem("ident_set")
        wk_in = sem("wk_in")
        wq_in = sem("wq_in")
        wv_in = sem("wv_in")
        biases_in = sem("biases_in")
        ctx_loaded = [sem(f"ctx_loaded{k}") for k in range(RING)]
        x_in = [sem(f"x_in{k}") for k in range(RING)]
        stored = [sem(f"stored{k}") for k in range(RING)]
        wT_turned = sem("wT_turned")
        wT_copied = sem("wT_copied")
        qk_done = sem("qk_done")
        qk_copied = sem("qk_copied")
        dots_done = sem("dots_done")
        half_set = sem("half_set")
        xT_turned = sem("xT_turned")
        xT_copied = sem("xT_copied")
        ctx_turned = sem("ctx_turned")
        ctx_copied = sem("ctx_copied")
        v_done = sem("v_done")
        v_copied = sem("v_copied")
        g_done = sem("g_done")
        g_copied = sem("g_copied")
        scores_done = sem("scores_done")
        max_done = sem("max_done")
        neg_done = sem("neg_done")
        bias_done = sem("bias_done")
        probs_done = sem("probs_done")
        rec_done = sem("rec_done")
        v_soft_done = sem("v_soft_done")
        pv_done = sem("pv_done")
        y_done = sem("y_done")
        stats_done = sem("stats_done")
        aggr_done = sem("aggr_done")
        var_ready = sem("var_ready")
        rstd_done = sem("rstd_done")
        shift_done = sem("shift_done")
        norm_done = sem("norm_done")
        pool_gamma = sem("pool_gamma")
        pool_out = sem("pool_out")
        dve_gamma = sem("dve_gamma")
        dve_out = sem("dve_out")

        def dma_count(b, k):
            return 4 * b - 4 * k + 16

        def slots(eng, slot):
            for s in range(LOOP_FROM):
                slot(s, s % RING)
            with eng.Fori(0, (LOOP_TO - LOOP_FROM) // RING) as turn:
                for i in range(RING):
                    slot(turn * RING + (LOOP_FROM + i), (LOOP_FROM + i) % RING)
            for s in range(LOOP_TO, B + 1):
                slot(s, s % RING)

        def is_in(s, low, high):
            return low <= s < high if isinstance(s, int) else True

        block = stack.enter_context(nc.Block())

        @block.sync
        def _(sp):
            sp.dma_start(wk_nat[:], Wk.rearrange("(c p) f -> p c f", p=P)).then_inc(wk_in, 16)
            sp.dma_start(wq_nat[:], Wq.rearrange("(c p) f -> p c f", p=P)).then_inc(wq_in, 16)

            def load_x(b, k):
                sp.dma_start(xbuf[:, k], x[bass.ds(b, 1)].rearrange("o (p j) e -> p (o j) e", j=RJ))\
                    .then_inc(x_in[k], 16)

            def load_ctx(b, k):
                sp.dma_start(ctx_nat[:, k], ctx_in[bass.ds(b, 1)].rearrange("o m l -> m (o l)"))\
                    .then_inc(ctx_loaded[k], 16)

            load_x(0, 0)
            load_ctx(0, 0)
            sp.dma_start(wv[:], Wv.rearrange("(c p) e -> p c e", p=P)).then_inc(wv_in, 16)
            load_ctx(1, 1)
            load_x(1, 1)

            def slot(s, k):
                kn = (k + 2) % RING
                if is_in(s, 2, B + 1):
                    sp.wait_ge(pool_out, s - 1)
                    sp.wait_ge(dve_out, s - 1)
                    sp.dma_start(out[bass.ds(s - 2, 1)].rearrange("o (p j) e -> p (o j) e", j=RJ),
                                 xbuf[:, kn]).then_inc(stored[kn], 16)
                if is_in(s, 2, B - 2):
                    sp.wait_ge(ctx_turned, s - 1)
                if is_in(s, 0, B - 2):
                    load_ctx(s + 2, kn)
                if is_in(s, 2, B - 2):
                    sp.wait_ge(stored[kn], dma_count(s - 2, kn))
                if is_in(s, 0, B - 2):
                    load_x(s + 2, kn)

            slots(sp, slot)
            k = (B - 1) % RING
            sp.wait_ge(pool_out, B)
            sp.wait_ge(dve_out, B)
            sp.dma_start(out[B - 1].rearrange("(p j) e -> p j e", j=RJ), xbuf[:, k]).then_inc(stored[k], 16)
            for b in range(B - RING, B):
                sp.wait_ge(stored[b % RING], dma_count(b, b % RING))

        @block.tensor
        def _(pe):
            pe.wait_ge(ident_set, 2)
            pe.wait_ge(wk_in, 16)
            for h, ps in enumerate((ctx_ps, v_ps)):
                for f in range(2 * h, 2 * h + 2):
                    for c in range(LC):
                        col = (f - 2 * h) * L + c * P
                        mm = pe.transpose(ps[:, col:col + P], wk_nat[:, c, f * P:(f + 1) * P], ident[:])
                mm.then_inc(wT_turned, 1)
            pe.wait_ge(wq_in, 16)
            qk_ps = (g_ps, s_ps)

            def turn_wq(f):
                if f >= 2:
                    pe.wait_ge(wT_copied, 2 + f - 1)
                for c in range(EC):
                    mm = pe.transpose(xT_ps[f % 2][:, c, :], wq_nat[:, c, f * P:(f + 1) * P], ident[:])
                mm.then_inc(wT_turned, 1)

            def multiply_qk(f):
                pe.wait_ge(wT_copied, 2 + f + 1)
                for c in range(LC):
                    mm = pe.matmul(qk_ps[c][:], wkT[:, f, c * P:(c + 1) * P], wqT[:, f, :],
                                   start=(f == 0), stop=(f == FC - 1))
                return mm

            turn_wq(0)
            turn_wq(1)
            multiply_qk(0)
            turn_wq(2)
            multiply_qk(1)
            turn_wq(3)
            multiply_qk(2)
            multiply_qk(3).then_inc(qk_done, 1)

            def turn_ctx(b, k):
                if is_in(b, 1, B):
                    pe.wait_ge(ctx_copied, b)
                pe.wait_ge(ctx_loaded[k], dma_count(b, k))
                for c in range(LC):
                    mm = pe.transpose(ctxT_v[:, c, :], ctx_nat[:, k, c * P:(c + 1) * P], ident[0:M, 0:M])
                mm.then_inc(ctx_turned, 1)

            def context(b, k):
                pe.wait_ge(ctx_copied, b + 1)
                if is_in(b, 1, B):
                    pe.wait_ge(v_copied, b)
                for c in range(LC):
                    mm = pe.matmul(v_ps[0:M, :], ctxT[:, k % 2, c, :], wv[:, c, :],
                                   start=(c == 0), stop=(c == LC - 1))
                mm.then_inc(v_done, 1)
                if is_in(b, 1, B):
                    pe.wait_ge(g_copied, b)
                for e in range(EC):
                    for c in range(LC):
                        pe.matmul(g_v[:, e, :], qkT[:, c, e * P:(e + 1) * P], ctxT[:, k % 2, c, :],
                                  start=(c == 0), stop=(c == LC - 1))
                for c in range(LC):
                    mm = pe.matmul(ckey_v, ctxT[:, k % 2, c, :], w_col[:, c:c + 1],
                                   start=(c == 0), stop=(c == LC - 1))
                mm.then_inc(g_done, 1)

            pe.wait_ge(wT_copied, 1)
            turn_ctx(0, 0)
            pe.wait_ge(wv_in, 16)
            pe.wait_ge(qk_copied, 2)
            pe.wait_ge(dots_done, EC + LC + 1)
            context(0, 0)

            def turn_x(s, k, e):
                if is_in(s, 1, B) or e >= 2:
                    pe.wait_ge(xT_copied, EC * s + e - 1)
                for j in range(RJ):
                    mm = pe.transpose(xT_ps[e % 2][:, j, :], xbuf[:, k, j, e * P:(e + 1) * P], ident[:])
                mm.then_inc(xT_turned, 1)

            def product(b, j):
                if is_in(b, 1, B) or j >= 2:
                    pe.wait_ge(y_done, RJ * b + j - 1)
                pe.matmul(pv_ps[j % 2][:], probs[:, j * P:(j + 1) * P], v_soft[:],
                          start=True, stop=True).then_inc(pv_done, 1)

            def slot(s, k):
                main, last = is_in(s, 0, B), is_in(s, 1, B + 1)
                if main:
                    pe.wait_ge(x_in[k], dma_count(s, k))
                    turn_x(s, k, 0)
                    turn_x(s, k, 1)
                if last:
                    pe.wait_ge(v_soft_done, s)
                    product(s - 1, 0)
                if main:
                    turn_x(s, k, 2)
                if last:
                    product(s - 1, 1)
                if main:
                    turn_x(s, k, 3)
                if last:
                    product(s - 1, 2)
                    product(s - 1, 3)
                if is_in(s, 0, B - 1):
                    turn_ctx(s + 1, (k + 1) % RING)
                if main:
                    pe.wait_ge(g_copied, s + 1)
                    for e in range(EC):
                        pe.wait_ge(xT_copied, EC * s + e + 1)
                        mm = pe.matmul(s_ps[0:M, :], gT[:, e, :], xT[:, e, :], start=(e == 0), stop=(e == EC - 1))
                    mm.then_inc(scores_done, 1)
                if is_in(s, 0, B - 1):
                    context(s + 1, (k + 1) % RING)

            slots(pe, slot)

        @block.scalar
        def _(act):
            for row, to in ((bk, bk_all), (bq, bq_all), (bv, bv_all), (gamma, gamma_all), (beta, beta_all)):
                act.dma_start(to[:], row.partition_broadcast(P)).then_inc(biases_in, 16)
            act.wait_ge(wT_turned, 1)
            act.activation(wkT[:, 0:2, :], ctx_ps[:].rearrange("p (f l) -> p f l", l=L), ACT.Copy)\
                .then_inc(wT_copied, 1)
            act.wait_ge(wT_turned, 2)
            act.activation(wkT[:, 2:4, :], v_ps[:].rearrange("p (f l) -> p f l", l=L), ACT.Copy)\
                .then_inc(wT_copied, 1)
            for f in range(FC):
                act.wait_ge(wT_turned, 3 + f)
                act.activation(wqT[:, f, :].rearrange("p (c q) -> p c q", q=P), xT_ps[f % 2][:], ACT.Copy)\
                    .then_inc(wT_copied, 1)
            act.wait_ge(qk_done, 1)
            act.activation(qkT[:, 0, :], g_ps[:], ACT.Copy).then_inc(qk_copied, 1)
            act.activation(qkT[:, 1, :], s_ps[:], ACT.Copy).then_inc(qk_copied, 1)

            def copy_ctx(b, k):
                act.wait_ge(ctx_turned, b + 1)
                act.activation(ctxT[:, k % 2], ctxT_v, ACT.Copy).then_inc(ctx_copied, 1)

            copy_ctx(0, 0)

            def slot(s, k):
                if is_in(s, 0, B):
                    for e in range(EC):
                        act.wait_ge(xT_turned, EC * s + e + 1)
                        act.activation(xT[:, e, :].rearrange("p (j q) -> p j q", q=P), xT_ps[e % 2][:], ACT.Copy)\
                            .then_inc(xT_copied, 1)
                if is_in(s, 0, B - 1):
                    copy_ctx(s + 1, (k + 1) % RING)
                if is_in(s, 0, B):
                    act.wait_ge(bias_done, s + 1)
                    act.activation(probs[:], s_ps[0:M, :], ACT.Exp, bias=s_bias[:], scale=SCALE,
                                   accum_out=s_sum[:]).then_inc(probs_done, 1)
                    act.wait_ge(rec_done, s + 1)
                    act.wait_ge(v_copied, s + 1)
                    act.activation(v_soft[:], v_raw[:, k % 2], ACT.Copy, scale=s_rec[:]).then_inc(v_soft_done, 1)
                if is_in(s, 1, B + 1):
                    kb = (k - 1) % RING
                    act.wait_ge(shift_done, s)
                    for j in range(POOL_J):
                        act.activation(xbuf[:, kb, j, :], xbuf[:, kb, j, :], ACT.Identity,
                                       bias=shift[:, j:j + 1], scale=rstd[:, kb % 2, j:j + 1]).then_inc(norm_done, 1)

            slots(act, slot)

        @block.vector
        def _(dve):
            dve.memset(minus_half[:], -0.5).then_inc(half_set, 1)
            dve.wait_ge(biases_in, 5 * 16)
            dve.wait_ge(wk_in, 16)
            for c in range(LC):
                dve.scalar_tensor_tensor(dot_junk[:, c], wk_nat[:, c], 1.0, bq_all[:], ALU.mult, ALU.mult,
                                         accum_out=w_col[:, c:c + 1]).then_inc(dots_done, 1)
            dve.scalar_tensor_tensor(dot_junk[:, LC], bk_all[:], 1.0, bq_all[:], ALU.mult, ALU.mult,
                                     accum_out=d_col[:]).then_inc(dots_done, 1)
            dve.wait_ge(wq_in, 16)
            for c in range(EC):
                dve.scalar_tensor_tensor(dot_junk[:, LC + 1 + c], wq_nat[:, c], 1.0, bk_all[:], ALU.mult, ALU.mult,
                                         accum_out=u_col[:, c:c + 1]).then_inc(dots_done, 1)
            dve.wait_ge(dots_done, EC + LC + 1)

            def context(b, k):
                dve.wait_ge(v_done, b + 1)
                if is_in(b, 2, B):
                    dve.wait_ge(v_soft_done, b - 1)
                dve.tensor_tensor(v_raw[:, k % 2], v_ps[0:M, :], bv_all[0:M, :], ALU.add).then_inc(v_copied, 1)
                dve.wait_ge(g_done, b + 1)
                if is_in(b, 2, B):
                    dve.wait_ge(bias_done, b - 1)
                dve.tensor_scalar(c_key[:, k % 2], ckey_v, d_col[0:M, :], None, ALU.add)
                dve.tensor_tensor(gT[:], g_v, u_col[:].unsqueeze(2).broadcast_to([P, EC, M]), ALU.add)\
                    .then_inc(g_copied, 1)

            context(0, 0)

            def slot(s, k):
                kb = (k - 1) % RING
                if is_in(s, 1, B + 1):
                    for j in range(RJ):
                        dve.wait_ge(pv_done, RJ * (s - 1) + j + 1)
                        dve.tensor_tensor(xbuf[:, kb, j, :], pv_ps[j % 2][:], xbuf[:, kb, j, :], ALU.add)\
                            .then_inc(y_done, 1)
                        dve.wait_ge(y_done, RJ * (s - 1) + j + 1)
                        dve.bn_stats(stats[:, j, :], xbuf[:, kb, j, :]).then_inc(stats_done, 1)
                        if j:
                            dve.bn_aggr(mean_var[:, j - 1, :], stats[:, j - 1, :]).then_inc(aggr_done, 1)
                    if is_in(s, 2, B + 1):
                        dve.wait_ge(shift_done, s - 1)
                    dve.wait_ge(stats_done, RJ * s)
                    dve.wait_ge(aggr_done, RJ * s - 1)
                    for low, high in ((0, RJ - 1), (RJ - 1, RJ)):
                        if high == RJ:
                            dve.bn_aggr(mean_var[:, RJ - 1, :], stats[:, RJ - 1, :]).then_inc(aggr_done, 1)
                            dve.wait_ge(aggr_done, RJ * s)
                        dve.tensor_scalar(var_eps[:, low:high], mean_var[:, low:high, 1], EPS, None, ALU.add)\
                            .then_inc(var_ready, 1)
                        dve.tensor_scalar(neg_mean[:, low:high], mean_var[:, low:high, 0], -1.0, None, ALU.mult)\
                            .then_inc(var_ready, 1)
                if is_in(s, 0, B):
                    dve.wait_ge(scores_done, s + 1)
                    dve.tensor_reduce(s_max[:], s_ps[0:M, :], AX.X, ALU.max).then_inc(max_done, 1)
                    dve.wait_ge(max_done, s + 1)
                    dve.tensor_scalar(s_neg[:], s_max[:], c_key[:, k % 2], -SCALE, ALU.add, ALU.mult)\
                        .then_inc(neg_done, 1)
                    dve.wait_ge(neg_done, s + 1)
                    dve.tensor_scalar(s_bias[:], c_key[:, k % 2], SCALE, s_neg[:], ALU.mult, ALU.add)\
                        .then_inc(bias_done, 1)
                    dve.wait_ge(probs_done, s + 1)
                    dve.reciprocal(s_rec[:], s_sum[:]).then_inc(rec_done, 1)
                if is_in(s, 1, B + 1):
                    dve.wait_ge(rstd_done, s)
                    for j in range(POOL_J, RJ):
                        dve.scalar_tensor_tensor(xbuf[:, kb, j, :], xbuf[:, kb, j, :], neg_mean[:, j:j + 1],
                                                 gamma_all[:], ALU.add, ALU.mult).then_inc(dve_gamma, 1)
                    dve.wait_ge(dve_gamma, (RJ - POOL_J) * s)
                    for j in range(POOL_J, RJ):
                        last = dve.scalar_tensor_tensor(xbuf[:, kb, j, :], xbuf[:, kb, j, :],
                                                        rstd[:, kb % 2, j:j + 1], beta_all[:], ALU.mult, ALU.add)
                    last.then_inc(dve_out, 1)
                if is_in(s, 0, B - 1):
                    context(s + 1, (k + 1) % RING)

            slots(dve, slot)

        @block.gpsimd
        def _(pool):
            pool.memset(ident[:], 0.0).then_inc(ident_set, 1)
            pool.wait_ge(ident_set, 1)
            pool.affine_select(out=ident[:], in_=ident[:], compare_op=ALU.not_equal, fill=1.0, base=0,
                               pattern=[[-1, P]], channel_multiplier=1).then_inc(ident_set, 1)
            pool.wait_ge(half_set, 1)
            pool.wait_ge(biases_in, 5 * 16)

            def slot(s, k):
                if not is_in(s, 1, B + 1):
                    return
                kb = (k - 1) % RING
                pool.wait_ge(var_ready, 4 * s)
                if is_in(s, 2, B + 1):
                    pool.wait_ge(norm_done, POOL_J * (s - 1))
                pool.tensor_tensor(rstd[:, kb % 2], var_eps[:], minus_half[:], ALU.pow).then_inc(rstd_done, 1)
                pool.wait_ge(rstd_done, s)
                pool.tensor_tensor(shift[:], neg_mean[:], rstd[:, kb % 2], ALU.mult).then_inc(shift_done, 1)
                for j in range(POOL_J):
                    pool.wait_ge(norm_done, POOL_J * (s - 1) + j + 1)
                    pool.tensor_tensor(xbuf[:, kb, j, :], xbuf[:, kb, j, :], gamma_all[:], ALU.mult)\
                        .then_inc(pool_gamma, 1)
                pool.wait_ge(pool_gamma, POOL_J * s)
                pool.tensor_tensor(xbuf[:, kb, 0:POOL_J, :], xbuf[:, kb, 0:POOL_J, :],
                                   beta_all[:].unsqueeze(1).broadcast_to([P, POOL_J, E]), ALU.add)\
                    .then_inc(pool_out, 1)

            slots(pool, slot)


INPUTS = ["x", "ctx_512", "L0_xattn_Wq", "L0_xattn_bq", "L0_xattn_Wk", "L0_xattn_bk", "L0_xattn_Wv",
          "L0_xattn_bv", "L0_xattn_gamma", "L0_xattn_beta"]


def kernel(**inputs):
    import numpy as np
    import concourse.bacc as bacc
    from concourse.bass_utils import run_bass_kernel_spmd

    nc = bacc.Bacc("TRN2", target_bir_lowering=False, num_devices=1)
    arrays, args = {}, []
    for name in INPUTS:
        a = np.ascontiguousarray(inputs[name])
        arrays[f"in_{name}"] = a
        args.append(nc.dram_tensor(f"in_{name}", a.shape, mybir.dt.from_np(a.dtype), kind="ExternalInput").ap())
    out = nc.dram_tensor("out", arrays["in_x"].shape, F32, kind="ExternalOutput").ap()
    cross_attention(nc, *args, out)
    r = run_bass_kernel_spmd(nc, [arrays], core_ids=[0])
    return r.results[0]["out"]
```

```python
from contextlib import ExitStack

import concourse.bass as bass
from concourse import mybir

P = 128
F32 = mybir.dt.float32
F16 = mybir.dt.float16
I32 = mybir.dt.int32
ALU = mybir.AluOpType
ACT = mybir.ActivationFunctionType
AX = mybir.AxisListType

EPS = 1e-6
RING = 4
LOOP_FROM = 2
POOL_J = 3
LAST_POOL_J = (2, 2, 1)
SQUARE_J = 2
PROB_SCALE = 2.0 ** 15
HIGH, LOW = 0, 1
PASSES = ((HIGH, HIGH), (HIGH, LOW), (LOW, HIGH))
EXPONENT_MASK = 0x7F800000
SCALE_FIELD = 127 + 127 + 14
BACK_FIELD = 14
LEAST_BOUND = 2.0 ** -100
CTX_PARTS = 4
WK, WQ, WV = CTX_PARTS, CTX_PARTS + 1, CTX_PARTS + 2


def cross_attention(nc, x, ctx_in, Wq, bq, Wk, bk, Wv, bv, gamma, beta, out):
    B, T, E = x.shape
    _, M, L = ctx_in.shape
    RJ = T // P
    EC = E // P
    FC = Wq.shape[1] // P
    LC = L // P
    SCALE = float(E) ** -0.5
    assert T == RJ * P and E == EC * P and L == LC * P and M <= P and EC * M + 1 <= 512
    assert LC == 2 and FC == 4 and EC == 4 and B * L <= 2 * RJ * E

    with ExitStack() as stack:
        def sb(name, shape, dt=F32):
            return stack.enter_context(nc.sbuf_tensor(name, shape, dt))

        def bank(name, shape, dt=F32):
            return stack.enter_context(nc.psum_tensor(name, shape, dt))

        def sem(name):
            return stack.enter_context(nc.semaphore(name))

        ident = sb("ident", [P, P])
        wq_nat = sb("wq_nat", [P, EC, E])
        wk_nat = sb("wk_nat", [P, LC, E])
        wqT = sb("wqT", [P, FC, E])
        wkT = sb("wkT", [P, FC, L])
        wv = sb("wv", [P, LC, E])
        wv_part = sb("wv_part", [P, 2, LC, E], F16)
        qk_part = sb("qk_part", [P, 2, LC, E], F16)
        bq_all = sb("bq_all", [P, E])
        bk_all = sb("bk_all", [P, E])
        bv_all = sb("bv_all", [P, E])
        gamma_all = sb("gamma_all", [P, E])
        beta_all = sb("beta_all", [P, E])
        junk = sb("junk", [P, EC + LC + 1, E])
        act_junk = sb("act_junk", [P, B * L + LC * E], F16)
        act_warm = sb("act_warm", [P, RJ])
        u_col = sb("u_col", [P, EC])
        w_col = sb("w_col", [P, LC])
        d_col = sb("d_col", [P, 1])
        ones = sb("ones", [P, M])
        w_diag = sb("w_diag", [P, LC, P])
        w_row = sb("w_row", [M, L + 1])
        key_junk = sb("key_junk", [M, RING, L + 1])
        own_bound = sb("own_bound", [P, 7])
        max_bound = sb("max_bound", [P, 7])
        bv_bound = sb("bv_bound", [P, 1])
        bound = sb("bound", [P, 4])
        field = sb("field", [P, 4])
        scale = sb("scale", [P, 4])
        back = sb("back", [P, 4])
        back_g = sb("back_g", [P, 1])
        back_v = sb("back_v", [P, 1])
        onto_v = sb("onto_v", [P, 1])
        back_y = sb("back_y", [P, 1])
        bv_scaled = sb("bv_scaled", [P, E])
        ctx_nat = sb("ctx_nat", [M, RING, L + 1])
        ctxT = sb("ctxT", [P, 2, 2, LC, M], F16)
        xbuf = sb("xbuf", [P, RING, RJ, E])
        obuf = sb("obuf", [P, 2, RJ, E])
        xT = sb("xT", [P, EC, T])
        gT = sb("gT", [P, 2, EC, M])
        c_key = sb("c_key", [M, RING, 1])
        probs = sb("probs", [M, T])
        prob_part = sb("prob_part", [M, 2, T], F16)
        v_scaled = sb("v_scaled", [M, 2, E])
        v_part = sb("v_part", [M, 2, 2, E], F16)
        s_max = sb("s_max", [M, 1])
        s_neg = sb("s_neg", [M, 1])
        s_bias = sb("s_bias", [M, 1])
        s_sum = sb("s_sum", [M, 1])
        s_rec = sb("s_rec", [M, 1])
        s_by = sb("s_by", [M, 1])
        stats = sb("stats", [P, RJ, 6])
        mean_var = sb("mean_var", [P, RJ, 2])
        square_junk = sb("square_junk", [P, RJ, E])
        y_sum = sb("y_sum", [P, RJ])
        square_sum = sb("square_sum", [P, RJ])
        square_mean = sb("square_mean", [P, RJ])
        one_over_e = sb("one_over_e", [P, RJ])
        eps_all = sb("eps_all", [P, RJ])
        minus_half = sb("minus_half", [P, RJ])
        var_eps = sb("var_eps", [P, RJ])
        neg_mean = sb("neg_mean", [P, RJ])
        rstd = sb("rstd", [P, RJ])
        shift = sb("shift", [P, POOL_J])

        xT_ps = [bank(f"xT_ps{i}", [P, RJ, P]) for i in range(2)]
        ctx_ps = bank("ctx_ps", [P, 512])
        v_ps = bank("v_ps", [P, 512])
        g_ps = bank("g_ps", [P, 512])
        s_ps = bank("s_ps", [P, 512])
        pv_ps = [bank(f"pv_ps{i}", [P, 512]) for i in range(2)]
        y_ps = (pv_ps[0], pv_ps[1], v_ps, pv_ps[0])
        ctxT_v = ctx_ps[:, 0:LC * M].rearrange("p (c m) -> p c m", m=M)
        g_v = g_ps[:, 0:EC * M].rearrange("p (c m) -> p c m", m=M)
        w_ps = v_ps[0:M, 0:L]
        ctx_all = obuf[0:M].rearrange("m q j e -> m (q j e)")[:, 0:B * L]

        ident_set = sem("ident_set")
        bound_cleared = sem("bound_cleared")
        wk_in = sem("wk_in")
        wq_in = sem("wq_in")
        wv_in = sem("wv_in")
        ctx_all_in = [sem(f"ctx_all_in{h}") for h in range(2)]
        bqk_in = sem("bqk_in")
        bv_in = sem("bv_in")
        norm_in = sem("norm_in")
        ctx_loaded = [sem(f"ctx_loaded{k}") for k in range(RING)]
        x_in = [sem(f"x_in{k}") for k in range(RING)]
        obuf_free = [sem(f"obuf_free{q}") for q in range(2)]
        wT_turned = sem("wT_turned")
        wT_copied = sem("wT_copied")
        qk_done = sem("qk_done")
        act_bounds = sem("act_bounds")
        dve_bounds = sem("dve_bounds")
        max_bounds = sem("max_bounds")
        scales_step = sem("scales_step")
        scales_done = sem("scales_done")
        back_done = sem("back_done")
        high_split = sem("high_split")
        low_split = sem("low_split")
        dots_done = sem("dots_done")
        ones_set = sem("ones_set")
        w_diag_done = sem("w_diag_done")
        w_spread = sem("w_spread")
        w_row_done = sem("w_row_done")
        key_done = sem("key_done")
        constants_set = sem("constants_set")
        xT_turned = sem("xT_turned")
        xT_copied = sem("xT_copied")
        ctx_turned = sem("ctx_turned")
        ctx_high = sem("ctx_high")
        ctx_low = sem("ctx_low")
        v_done = sem("v_done")
        v_copied = sem("v_copied")
        g_done = sem("g_done")
        g_copied = sem("g_copied")
        scores_done = sem("scores_done")
        max_done = sem("max_done")
        neg_done = sem("neg_done")
        bias_done = sem("bias_done")
        probs_done = sem("probs_done")
        rec_done = sem("rec_done")
        by_done = sem("by_done")
        prob_high = sem("prob_high")
        prob_low = sem("prob_low")
        v_high = sem("v_high")
        v_low = sem("v_low")
        pv_done = sem("pv_done")
        y_done = sem("y_done")
        stats_done = sem("stats_done")
        aggr_done = sem("aggr_done")
        var_ready = sem("var_ready")
        sums_negated = sem("sums_negated")
        mean_negated = sem("mean_negated")
        squares_done = sem("squares_done")
        square_mean_done = sem("square_mean_done")
        rstd_done = sem("rstd_done")
        shift_done = sem("shift_done")
        norm_done = sem("norm_done")
        pool_gamma = sem("pool_gamma")
        pool_out = sem("pool_out")
        dve_gamma = sem("dve_gamma")
        dve_out = sem("dve_out")
        tail_out = [sem(f"tail_out{j}") for j in range(RJ)]
        tail_stored = sem("tail_stored")

        def slots(eng, slot, loop_from=LOOP_FROM, end=B + 2):
            loop_to = loop_from + (B - 2 - loop_from) // RING * RING
            for s in range(loop_from):
                slot(s, s % RING, s // RING)
            with eng.Fori(0, (loop_to - loop_from) // RING) as turn:
                for i in range(loop_from, loop_from + RING):
                    slot(turn * RING + i, i % RING, turn + i // RING)
            for s in range(loop_to, end):
                slot(s, s % RING, s // RING)

        def is_in(s, low, high):
            return low <= s < high if isinstance(s, int) else True

        def obuf_fills(k, r):
            return 16 * (r * (RING // 2) + (k - 2) // 2 + 1)

        def is_slot(s, which):
            return isinstance(s, int) and s == which

        def pool_share(s):
            return LAST_POOL_J[s - B + 1] if isinstance(s, int) and s >= B - 1 else POOL_J

        def moved(s):
            return sum(POOL_J - share for share in LAST_POOL_J[:s - B + 1]) if isinstance(s, int) and s >= B else 0

        block = stack.enter_context(nc.Block())

        @block.sync
        def _(sp):
            def load_x(b, k):
                sp.dma_start(xbuf[:, k], x[bass.ds(b, 1)].rearrange("o (p j) e -> p (o j) e", j=RJ))\
                    .then_inc(x_in[k], 16)

            def load_ctx(b, k):
                sp.dma_start(ctx_nat[:, k, 0:L], ctx_in[bass.ds(b, 1)].rearrange("o m l -> m (o l)"))\
                    .then_inc(ctx_loaded[k], 16)

            sp.dma_start(wk_nat[:], Wk.rearrange("(c p) f -> p c f", p=P)).then_inc(wk_in, 16)
            sp.dma_start(wq_nat[:], Wq.rearrange("(c p) f -> p c f", p=P)).then_inc(wq_in, 16)
            load_ctx(0, 0)
            all_v = ctx_all.rearrange("m (b l) -> m b l", l=L)
            for h in range(2):
                sp.dma_start(all_v[:, h * B // 2:(h + 1) * B // 2],
                             ctx_in[h * B // 2:(h + 1) * B // 2].rearrange("b m l -> m b l"))\
                    .then_inc(ctx_all_in[h], 16)
            sp.dma_start(wv[:], Wv.rearrange("(c p) e -> p c e", p=P)).then_inc(wv_in, 16)
            load_ctx(1, 1)
            load_x(0, 0)
            sp.dma_start(bv_all[:], bv.partition_broadcast(P)).then_inc(bv_in, 16)

            def slot(s, k, r):
                if is_in(s, 2, B - 2):
                    sp.wait_ge(ctx_turned, s - 1)
                    sp.wait_ge(key_done, s - 1)
                if is_in(s, 0, B - 2):
                    load_ctx(s + 2, (k + 2) % RING)
                if is_in(s, 3, B - 1):
                    sp.wait_ge(norm_done, POOL_J * (s - 2))
                    sp.wait_ge(dve_gamma, (RJ - POOL_J) * (s - 2))
                if is_in(s, 0, B - 1):
                    load_x(s + 1, (k + 1) % RING)
                if is_slot(s, 0):
                    sp.dma_start(gamma_all[:], gamma.partition_broadcast(P)).then_inc(norm_in, 16)
                    sp.dma_start(beta_all[:], beta.partition_broadcast(P)).then_inc(norm_in, 16)
                if is_in(s, 3, B + 2):
                    sp.wait_ge(pool_out, s - 2)
                    sp.wait_ge(dve_out, s - 2)
                    sp.dma_start(out[bass.ds(s - 3, 1)].rearrange("o (p j) e -> p (o j) e", j=RJ),
                                 obuf[:, (k + 1) % 2]).then_inc(obuf_free[(k + 1) % 2], 16)

            slots(sp, slot, loop_from=3)
            for j in (*range(LAST_POOL_J[-1], RJ), *range(LAST_POOL_J[-1])):
                sp.wait_ge(tail_out[j], 1)
                sp.dma_start(out[B - 1].rearrange("(p j) e -> p j e", j=RJ)[:, j], obuf[:, (B - 1) % 2, j])\
                    .then_inc(tail_stored, 16)
            sp.wait_ge(obuf_free[0], 16 * (B // 2 + 1))
            sp.wait_ge(obuf_free[1], 16 * (B // 2))
            sp.wait_ge(tail_stored, 16 * RJ)

        @block.tensor
        def _(pe):
            def keep_warm(n, ps):
                for _ in range(n):
                    pe.transpose(ps[:, 0:P], ident[:], ident[:])

            pe.wait_ge(ident_set, 2)
            keep_warm(12, g_ps)
            pe.wait_ge(wk_in, 16)
            for h, ps in enumerate((ctx_ps, v_ps)):
                for f in range(2 * h, 2 * h + 2):
                    for c in range(LC):
                        col = (f - 2 * h) * L + c * P
                        mm = pe.transpose(ps[:, col:col + P], wk_nat[:, c, f * P:(f + 1) * P], ident[:])
                mm.then_inc(wT_turned, 1)
            keep_warm(12, g_ps)
            pe.wait_ge(wq_in, 16)
            qk_ps = (g_ps, s_ps)

            def turn_wq(f):
                if f >= 2:
                    pe.wait_ge(wT_copied, 2 + f - 1)
                for c in range(EC):
                    mm = pe.transpose(xT_ps[f % 2][:, c, :], wq_nat[:, c, f * P:(f + 1) * P], ident[:])
                mm.then_inc(wT_turned, 1)

            def multiply_qk(f):
                pe.wait_ge(wT_copied, 2 + f + 1)
                for c in range(LC):
                    mm = pe.matmul(qk_ps[c][:], wkT[:, f, c * P:(c + 1) * P], wqT[:, f, :],
                                   start=(f == 0), stop=(f == FC - 1))
                    if f == FC - 1:
                        mm.then_inc(qk_done, 1)

            def turn_ctx(b, k, r):
                if is_in(b, 1, B):
                    pe.wait_ge(ctx_low, b)
                pe.wait_ge(ctx_loaded[k], 16 * (r + 1))
                for c in range(LC):
                    mm = pe.transpose(ctxT_v[:, c, :], ctx_nat[:, k, c * P:(c + 1) * P], ident[0:M, 0:M])
                mm.then_inc(ctx_turned, 1)

            def context_v(b, k):
                pe.wait_ge(ctx_low, b + 1)
                if is_in(b, 1, B):
                    pe.wait_ge(v_copied, b)
                if is_in(b, 3, B):
                    pe.wait_ge(y_done, RJ * (b - 3) + 3)
                steps = [(c, *parts) for c in range(LC) for parts in PASSES]
                for n, (c, of_ctx, of_w) in enumerate(steps):
                    mm = pe.matmul(v_ps[0:M, :], ctxT[:, k % 2, of_ctx, c, :], wv_part[:, of_w, c, :],
                                   start=(n == 0), stop=(n == len(steps) - 1))
                mm.then_inc(v_done, 1)

            def context_g(b, k, half):
                if half == 0:
                    pe.wait_ge(ctx_low, b + 1)
                if half == 0 and is_in(b, 1, B):
                    pe.wait_ge(g_copied, EC * b)
                steps = [(c, *parts) for c in range(LC) for parts in PASSES]
                for e in range(half * EC // 2, (half + 1) * EC // 2):
                    for n, (c, of_w, of_ctx) in enumerate(steps):
                        mm = pe.matmul(g_v[:, e, :], qk_part[:, of_w, c, e * P:(e + 1) * P],
                                       ctxT[:, k % 2, of_ctx, c, :], start=(n == 0), stop=(n == len(steps) - 1))
                if half == 1:
                    mm.then_inc(g_done, 1)

            def turn_x(s, k, e):
                if is_in(s, 1, B) or e >= 2:
                    pe.wait_ge(xT_copied, EC * s + e - 1)
                for j in range(RJ):
                    mm = pe.transpose(xT_ps[e % 2][:, j, :], xbuf[:, k, j, e * P:(e + 1) * P], ident[:])
                mm.then_inc(xT_turned, 1)

            def product(b, k, j):
                if j == 0 and is_in(b, 1, B):
                    pe.wait_ge(y_done, RJ * b)
                if j == 2 and is_in(b, 0, B - 2):
                    pe.wait_ge(v_copied, b + 3)
                if j == 3:
                    pe.wait_ge(y_done, RJ * b + 1)
                for n, (of_p, of_v) in enumerate(PASSES):
                    if j == 0 and n == len(PASSES) - 1:
                        pe.wait_ge(prob_low, b + 1)
                    mm = pe.matmul(y_ps[j][:], prob_part[:, of_p, j * P:(j + 1) * P], v_part[:, k % 2, of_v, :],
                                   start=(n == 0), stop=(n == len(PASSES) - 1))
                mm.then_inc(pv_done, 1)

            def scores(s, k):
                for e in range(EC):
                    pe.wait_ge(g_copied, EC * s + e + 1)
                    pe.wait_ge(xT_copied, EC * s + e + 1)
                    mm = pe.matmul(s_ps[0:M, :], gT[:, k % 2, e, :], xT[:, e, :],
                                   start=(e == 0), stop=(e == EC - 1))
                mm.then_inc(scores_done, 1)

            turn_wq(0)
            turn_wq(1)
            multiply_qk(0)
            turn_wq(2)
            multiply_qk(1)
            pe.wait_ge(wT_copied, 1)
            turn_ctx(0, 0, 0)
            turn_wq(3)
            pe.wait_ge(wT_copied, 2)
            pe.wait_ge(ones_set, 1)
            pe.wait_ge(w_diag_done, LC)
            for c in range(LC):
                mm = pe.matmul(w_ps[:, c * P:(c + 1) * P], ones[:], w_diag[:, c, :], start=True, stop=True)
            mm.then_inc(w_spread, 1)
            multiply_qk(2)
            multiply_qk(3)
            keep_warm(14, pv_ps[0])
            pe.wait_ge(wT_copied, 2 + FC)
            pe.wait_ge(x_in[0], 16)
            turn_x(0, 0, 0)
            turn_x(0, 0, 1)
            pe.wait_ge(high_split, 2)
            pe.wait_ge(low_split, 2)
            context_g(0, 0, 0)
            context_g(0, 0, 1)
            turn_x(0, 0, 2)
            turn_x(0, 0, 3)
            turn_ctx(1, 1, 0)
            scores(0, 0)
            context_g(1, 1, 0)
            context_g(1, 1, 1)
            pe.wait_ge(high_split, 3)
            pe.wait_ge(low_split, 3)
            context_v(0, 0)
            turn_ctx(2, 2, 0)

            def slot(s, k, r):
                if is_slot(s, 0):
                    return
                main, last = is_in(s, 0, B), is_in(s, 1, B + 1)
                more = is_in(s, 0, B - 1)
                k1 = (k + 1) % RING
                if main:
                    pe.wait_ge(x_in[k], 16 * (r + 1))
                    turn_x(s, k, 0)
                    turn_x(s, k, 1)
                if is_slot(s, 1):
                    context_v(1, 1)
                elif more:
                    context_v(s + 1, k1)
                if main:
                    turn_x(s, k, 2)
                    turn_x(s, k, 3)
                if more:
                    context_g(s + 1, k1, 0)
                    context_g(s + 1, k1, 1)
                if is_slot(s, 1):
                    context_v(2, 2)
                if is_slot(s, B):
                    pe.wait_ge(y_done, RJ * (B - 1))
                    keep_warm(26, pv_ps[0])
                if last:
                    pe.wait_ge(v_low, s)
                    pe.wait_ge(prob_high, s)
                    product(s - 1, k + 1, 0)
                    product(s - 1, k + 1, 1)
                    product(s - 1, k + 1, 2)
                if is_in(s, 0, B - 2):
                    turn_ctx(s + 2, (k + 2) % RING, r + (k + 2) // RING)
                if last:
                    product(s - 1, k + 1, 3)
                if main:
                    scores(s, k)

            slots(pe, slot)

        @block.scalar
        def _(act):
            act.dma_start(bq_all[:], bq.partition_broadcast(P)).then_inc(bqk_in, 16)
            act.dma_start(bk_all[:], bk.partition_broadcast(P)).then_inc(bqk_in, 16)
            act.wait_ge(constants_set, 3)
            act.activation(act_warm[:], eps_all[:], ACT.Copy)
            act.wait_ge(wT_turned, 1)
            act.activation(wkT[:, 0:2, :], ctx_ps[:].rearrange("p (f l) -> p f l", l=L), ACT.Copy)\
                .then_inc(wT_copied, 1)
            act.wait_ge(wT_turned, 2)
            act.activation(wkT[:, 2:4, :], v_ps[:].rearrange("p (f l) -> p f l", l=L), ACT.Copy)\
                .then_inc(wT_copied, 1)
            act.wait_ge(bound_cleared, 1)
            act.activation(act_junk[:, B * L:B * L + LC * E].rearrange("p (c e) -> p c e", e=E), wk_nat[:], ACT.Abs,
                           accum_out=own_bound[:, WK:WK + 1]).then_inc(act_bounds, 1)
            part = B * L // CTX_PARTS

            def copy_wqT(f):
                act.wait_ge(wT_turned, 3 + f)
                act.activation(wqT[:, f, :].rearrange("p (c q) -> p c q", q=P), xT_ps[f % 2][:], ACT.Copy)\
                    .then_inc(wT_copied, 1)

            def sum_ctx(h):
                act.wait_ge(ctx_all_in[h * 2 // CTX_PARTS], 16)
                act.activation(act_junk[0:M, h * part:(h + 1) * part], ctx_all[:, h * part:(h + 1) * part], ACT.Abs,
                               accum_out=own_bound[0:M, h:h + 1]).then_inc(act_bounds, 1)

            copy_wqT(0)
            copy_wqT(1)
            sum_ctx(0)
            copy_wqT(2)
            sum_ctx(1)
            copy_wqT(3)
            sum_ctx(2)
            act.wait_ge(scales_done, 1)
            def ctx_to_high(b, k):
                act.wait_ge(ctx_turned, b + 1)
                if is_in(b, 2, B):
                    act.wait_ge(g_done, b - 1)
                act.activation(ctxT[:, k % 2, HIGH], ctxT_v, ACT.Copy, scale=scale[:, 0:1]).then_inc(ctx_high, 1)

            def copy_xT(s, e):
                act.wait_ge(xT_turned, EC * s + e + 1)
                act.activation(xT[:, e, :].rearrange("p (j q) -> p j q", q=P), xT_ps[e % 2][:], ACT.Copy)\
                    .then_inc(xT_copied, 1)

            def copy_g(b, k):
                act.wait_ge(g_done, b + 1)
                for e in range(EC):
                    act.activation(gT[:, k % 2, e, :], g_v[:, e, :], ACT.Identity, scale=back_g[:],
                                   bias=u_col[:, e:e + 1]).then_inc(g_copied, 1)

            ctx_to_high(0, 0)
            for c in range(LC):
                act.wait_ge(qk_done, c + 1)
                act.activation(qk_part[:, HIGH, c, :], (g_ps, s_ps)[c][:], ACT.Copy, scale=scale[:, 1:2])\
                    .then_inc(high_split, 1)
            copy_xT(0, 0)
            copy_xT(0, 1)
            act.wait_ge(back_done, 1)
            act.wait_ge(dots_done, LC + 1 + EC)
            copy_g(0, 0)
            copy_xT(0, 2)
            copy_xT(0, 3)
            ctx_to_high(1, 1)
            act.wait_ge(scales_done, 2)
            act.activation(wv_part[:, HIGH], wv[:], ACT.Copy, scale=scale[:, 2:3]).then_inc(high_split, 1)

            def slot(s, k, r):
                kb, kn = (k - 1) % RING, (k - 2) % RING
                main = is_in(s, 1, B)

                def v_to_high(b):
                    act.wait_ge(v_copied, b + 1)
                    if is_in(b, 2, B):
                        act.wait_ge(pv_done, RJ * (b - 1))
                    act.activation(v_part[:, b % 2 if isinstance(b, int) else k % 2, HIGH],
                                   v_scaled[:, b % 2 if isinstance(b, int) else k % 2], ACT.Copy).then_inc(v_high, 1)

                if is_in(s, 2, B):
                    v_to_high(s)
                if main:
                    copy_xT(s, 0)
                    copy_xT(s, 1)
                if is_in(s, 1, B + 1):
                    act.wait_ge(bias_done, s)
                    act.activation(probs[:], s_ps[0:M, :], ACT.Exp, bias=s_bias[:], scale=SCALE,
                                   accum_out=s_sum[:]).then_inc(probs_done, 1)
                    if is_slot(s, 1):
                        ctx_to_high(2, 2)
                    act.wait_ge(by_done, s)
                    act.activation(prob_part[:, HIGH], probs[:], ACT.Copy, scale=s_by[:]).then_inc(prob_high, 1)
                if is_slot(s, 1):
                    v_to_high(0)
                if is_in(s, 2, B + 2):
                    act.wait_ge(shift_done, s - 1)
                    act.wait_ge(obuf_free[k % 2], obuf_fills(k, r))
                    for j in range(pool_share(s)):
                        act.activation(obuf[:, k % 2, j, :], xbuf[:, kn, j, :], ACT.Identity,
                                       bias=shift[:, j:j + 1], scale=rstd[:, j:j + 1]).then_inc(norm_done, 1)
                if main:
                    copy_xT(s, 2)
                    copy_xT(s, 3)
                if is_slot(s, 1):
                    v_to_high(1)
                if is_in(s, 1, B - 2):
                    ctx_to_high(s + 2, k + 2)
                if is_in(s, 0, B - 1):
                    copy_g(s + 1, k + 1)
                if is_in(s, 1, B + 1):
                    act.wait_ge(sums_negated, s)
                    for j in range(RJ if is_slot(s, B) else SQUARE_J):
                        if is_slot(s, B) and j:
                            act.wait_ge(sums_negated, s + j)
                        act.activation(square_junk[:, j], xbuf[:, kb, j, :], ACT.Square, bias=neg_mean[:, j:j + 1],
                                       accum_out=square_sum[:, j:j + 1]).then_inc(squares_done, 1)

            slots(act, slot)

        @block.vector
        def _(dve):
            dve.memset(own_bound[:], 0.0).then_inc(bound_cleared, 1)
            dve.memset(minus_half[:], -0.5).then_inc(constants_set, 1)
            dve.memset(eps_all[:], EPS).then_inc(constants_set, 1)
            dve.memset(one_over_e[:], 1.0 / E).then_inc(constants_set, 1)

            def largest(out_, in_):
                dve.tensor_reduce(out_, in_, AX.X, ALU.max, apply_absolute_value=True).then_inc(dve_bounds, 1)

            def dot(n, in_, bias_row, out_):
                dve.scalar_tensor_tensor(junk[:, n], in_, 1.0, bias_row[:], ALU.mult, ALU.mult, accum_out=out_)\
                    .then_inc(dots_done, 1)

            dve.wait_ge(bqk_in, 2 * 16)
            dot(LC + EC, bk_all[:], bq_all, d_col[:])
            dve.wait_ge(wk_in, 16)
            for c in range(LC):
                dot(c, wk_nat[:, c], bq_all, w_col[:, c:c + 1])
            dve.wait_ge(ident_set, 2)
            dve.wait_ge(dots_done, LC + 1)
            for c in range(LC):
                dve.tensor_scalar(w_diag[:, c, :], ident[:], w_col[:, c:c + 1], None, ALU.mult).then_inc(w_diag_done, 1)
            dve.tensor_copy(w_row[:, L:L + 1], d_col[0:M, :])
            dve.wait_ge(wq_in, 16)
            dve.wait_ge(bound_cleared, 1)
            largest(own_bound[:, WQ:WQ + 1], wq_nat[:].rearrange("p c e -> p (c e)"))
            dot(LC, wq_nat[:, 0], bk_all, u_col[:, 0:1])
            dve.wait_ge(ctx_all_in[1], 16)
            dve.tensor_reduce(own_bound[0:M, CTX_PARTS - 1:CTX_PARTS], ctx_all[:, (CTX_PARTS - 1) * B * L // CTX_PARTS:],
                              AX.X, ALU.add, apply_absolute_value=True).then_inc(dve_bounds, 1)
            dve.wait_ge(wv_in, 16)
            dot(LC + 1, wq_nat[:, 1], bk_all, u_col[:, 1:2])
            step = 0

            def scales(instruction):
                nonlocal step
                step += 1
                instruction.then_inc(scales_step, 1)
                dve.wait_ge(scales_step, step)

            def exact_scales(low, high):
                scales(dve.tensor_scalar(bound[:, low:high], bound[:, low:high], LEAST_BOUND, None, ALU.max))
                scales(dve.tensor_scalar(field[:, low:high].bitcast(I32), bound[:, low:high].bitcast(I32),
                                         EXPONENT_MASK, None, ALU.bitwise_and))
                dve.tensor_scalar(scale[:, low:high].bitcast(I32), field[:, low:high].bitcast(I32), -1.0,
                                  float(SCALE_FIELD << 23), ALU.mult, ALU.add).then_inc(scales_done, 1)
                scales(dve.tensor_scalar(back[:, low:high].bitcast(I32), field[:, low:high].bitcast(I32),
                                         float(BACK_FIELD << 23), None, ALU.subtract))

            dve.wait_ge(max_bounds, 1)
            dve.tensor_reduce(bound[:, 0:1], max_bound[:, 0:CTX_PARTS], AX.X, ALU.max)
            scales(dve.tensor_tensor(bound[:, 1:2], max_bound[:, WQ:WQ + 1], max_bound[:, WK:WK + 1], ALU.mult))
            exact_scales(0, 2)
            dve.tensor_tensor(back_g[:], back[:, 0:1], back[:, 1:2], ALU.mult).then_inc(back_done, 1)
            dve.wait_ge(scales_done, 1)

            def low_part(out_, in_, by, high, n):
                dve.wait_ge(high_split, n)
                dve.scalar_tensor_tensor(out_, in_, by, high, ALU.mult, ALU.subtract).then_inc(low_split, 1)

            def ctx_to_low(b, k):
                dve.wait_ge(ctx_high, b + 1)
                dve.scalar_tensor_tensor(ctxT[:, k % 2, LOW], ctxT_v, scale[:, 0:1], ctxT[:, k % 2, HIGH],
                                         ALU.mult, ALU.subtract).then_inc(ctx_low, 1)

            ctx_to_low(0, 0)
            dve.wait_ge(w_spread, 1)
            dve.tensor_copy(w_row[:, 0:L], w_ps).then_inc(w_row_done, 1)
            low_part(qk_part[:, LOW, 0, :], g_ps[:], scale[:, 1:2], qk_part[:, HIGH, 0, :], 1)
            low_part(qk_part[:, LOW, 1, :], s_ps[:], scale[:, 1:2], qk_part[:, HIGH, 1, :], 2)
            for c in range(2, EC):
                dot(LC + c, wq_nat[:, c], bk_all, u_col[:, c:c + 1])
            dve.wait_ge(wv_in, 16)
            largest(own_bound[:, WV:WV + 1], wv[:].rearrange("p c e -> p (c e)"))
            dve.wait_ge(bv_in, 16)
            largest(bv_bound[:], bv_all[:])
            dve.wait_ge(max_bounds, 2)
            dve.tensor_copy(bound[:, 2:3], max_bound[:, WV:WV + 1])
            dve.wait_ge(dve_bounds, 4)
            scales(dve.scalar_tensor_tensor(bound[:, 3:4], bound[:, 0:1], max_bound[:, WV:WV + 1], bv_bound[:],
                                            ALU.mult, ALU.add))
            exact_scales(2, 4)
            dve.wait_ge(scales_done, 2)
            dve.tensor_scalar(back_y[:], back[:, 3:4], 1.0 / PROB_SCALE, None, ALU.mult)
            dve.tensor_scalar(bv_scaled[:], bv_all[:], scale[:, 3:4], None, ALU.mult)
            scales(dve.tensor_tensor(back_v[:], back[:, 0:1], back[:, 2:3], ALU.mult))
            ctx_to_low(1, 1)
            dve.tensor_tensor(onto_v[:], back_v[:], scale[:, 3:4], ALU.mult)
            low_part(wv_part[:, LOW], wv[:], scale[:, 2:3], wv_part[:, HIGH], 3)
            dve.wait_ge(low_split, 3)

            def key_bias(b, k, r):
                dve.wait_ge(ctx_loaded[k], 16 * (r + 1))
                dve.scalar_tensor_tensor(key_junk[:, k], ctx_nat[:, k], 1.0, w_row[:], ALU.mult, ALU.mult,
                                         accum_out=c_key[:, k]).then_inc(key_done, 1)

            dve.wait_ge(w_row_done, 1)
            dve.wait_ge(ones_set, 2)
            key_bias(0, 0, 0)
            key_bias(1, 1, 0)

            def copy_v(b, k):
                dve.wait_ge(v_done, b + 1)
                if is_in(b, 2, B):
                    dve.wait_ge(v_low, b - 1)
                dve.scalar_tensor_tensor(v_scaled[:, k % 2], v_ps[0:M, :], onto_v[0:M, :], bv_scaled[0:M, :],
                                         ALU.mult, ALU.add).then_inc(v_copied, 1)


            def slot(s, k, r):
                kb, kn = (k - 1) % RING, (k - 2) % RING
                softmax, finish = is_in(s, 1, B + 1), is_in(s, 2, B + 2)
                groups = range(pool_share(s), RJ)

                def probs_to_low():
                    dve.wait_ge(prob_high, s)
                    dve.scalar_tensor_tensor(prob_part[:, LOW], probs[:], s_by[:], prob_part[:, HIGH],
                                             ALU.mult, ALU.subtract).then_inc(prob_low, 1)

                if softmax:
                    dve.wait_ge(key_done, s)
                    dve.wait_ge(scores_done, s)
                    dve.tensor_reduce(s_max[:], s_ps[0:M, :], AX.X, ALU.max).then_inc(max_done, 1)
                    dve.wait_ge(max_done, s)
                    dve.tensor_scalar(s_neg[:], s_max[:], c_key[:, (k - 1) % RING], -SCALE, ALU.add, ALU.mult)\
                        .then_inc(neg_done, 1)
                    dve.wait_ge(neg_done, s)
                    dve.tensor_scalar(s_bias[:], c_key[:, (k - 1) % RING], SCALE, s_neg[:], ALU.mult, ALU.add)\
                        .then_inc(bias_done, 1)
                late = is_slot(s, B - 1) or is_slot(s, B)

                def center(j):
                    if is_slot(s, B + 1):
                        dve.wait_ge(sums_negated, B - 1 + RJ)
                    else:
                        dve.wait_ge(aggr_done, (RJ - SQUARE_J) * (s - 1))
                        dve.wait_ge(mean_negated, s - 1)
                    dve.wait_ge(obuf_free[k % 2], obuf_fills(k, r))
                    if j < RJ - 1 or is_slot(s, B + 1):
                        by, op = neg_mean[:, j:j + 1], ALU.add
                    else:
                        by, op = mean_var[:, j, 0:1], ALU.subtract
                    dve.scalar_tensor_tensor(obuf[:, k % 2, j, :], xbuf[:, kn, j, :], by, gamma_all[:], op, ALU.mult)\
                        .then_inc(dve_gamma, 1)

                def rescale(j):
                    dve.wait_ge(rstd_done, s if is_slot(s, B + 1) and j >= 2 else s - 1)
                    dve.wait_ge(dve_gamma, (RJ - POOL_J) * (s - 2) + moved(s) + j - groups[0] + 1)
                    done = dve.scalar_tensor_tensor(obuf[:, k % 2, j, :], obuf[:, k % 2, j, :],
                                                    rstd[:, j:j + 1], beta_all[:], ALU.mult, ALU.add)
                    if not is_in(s, 2, B + 1):
                        done.then_inc(tail_out[j], 1)
                    elif j == RJ - 1:
                        done.then_inc(dve_out, 1)

                if finish:
                    center(groups[0])
                    if not late:
                        for j in groups[1:]:
                            center(j)
                if is_slot(s, 1):
                    copy_v(0, 0)
                if softmax:
                    dve.wait_ge(probs_done, s)
                    dve.reciprocal(s_rec[:], s_sum[:]).then_inc(rec_done, 1)
                    dve.wait_ge(rec_done, s)
                    dve.tensor_scalar(s_by[:], s_rec[:], PROB_SCALE, None, ALU.mult).then_inc(by_done, 1)
                if is_slot(s, 1):
                    ctx_to_low(2, 2)
                    copy_v(1, 1)
                    dve.wait_ge(norm_in, 2 * 16)
                if finish:
                    if late:
                        for j in groups[1:]:
                            center(j)
                if is_in(s, 1, B - 1) and not is_slot(s, 1):
                    copy_v(s + 1, k + 1)
                if softmax:
                    probs_to_low()
                if is_slot(s, 1):
                    copy_v(2, 2)
                if finish:
                    for j in groups[0:1] if late else groups:
                        rescale(j)

                def residual(j):
                    dve.wait_ge(pv_done, RJ * (s - 1) + j + 1)
                    dve.scalar_tensor_tensor(xbuf[:, kb, j, :], y_ps[j][:], back_y[:], xbuf[:, kb, j, :], ALU.mult,
                                             ALU.add, accum_out=y_sum[:, j:j + 1] if j < SQUARE_J or is_slot(s, B) else None)\
                        .then_inc(y_done, 1)

                def statistics(j):
                    dve.wait_ge(y_done, RJ * (s - 1) + j + 1)
                    dve.bn_stats(stats[:, j, :], xbuf[:, kb, j, :]).then_inc(stats_done, 1)

                if softmax:
                    if is_in(s, 2, B + 1):
                        dve.wait_ge(shift_done, s - 1)
                    residual(0)
                    residual(1)
                if is_in(s, 1, B - 2):
                    ctx_to_low(s + 2, k + 2)
                if is_in(s, 0, B - 2):
                    key_bias(s + 2, (k + 2) % RING, r + (k + 2) // RING)
                if is_slot(s, B):
                    for j in range(RJ):
                        if j >= 2:
                            residual(j)
                        for done in (j - 1,) if 0 < j < RJ - 1 else (j - 1, j) if j == RJ - 1 else ():
                            dve.wait_ge(y_done, RJ * (B - 1) + done + 1)
                            dve.tensor_scalar(neg_mean[:, done:done + 1], y_sum[:, done:done + 1], -1.0 / E, None,
                                              ALU.mult).then_inc(sums_negated, 1)
                    for j in groups[1:]:
                        rescale(j)
                elif softmax:
                    residual(2)
                    dve.wait_ge(y_done, RJ * (s - 1) + SQUARE_J)
                    dve.tensor_scalar(neg_mean[:, 0:SQUARE_J], y_sum[:, 0:SQUARE_J], -1.0 / E, None, ALU.mult)\
                        .then_inc(sums_negated, 1)
                    residual(3)
                    statistics(2)
                    dve.wait_ge(stats_done, (RJ - SQUARE_J) * (s - 1) + 1)
                    statistics(3)
                    dve.bn_aggr(mean_var[:, 2, :], stats[:, 2, :]).then_inc(aggr_done, 1)
                    dve.wait_ge(stats_done, (RJ - SQUARE_J) * s)
                    dve.wait_ge(aggr_done, (RJ - SQUARE_J) * s - 1)
                    dve.tensor_scalar(neg_mean[:, 2:3], mean_var[:, 2:3, 0], -1.0, None, ALU.mult)\
                        .then_inc(mean_negated, 1)
                    dve.bn_aggr(mean_var[:, 3, :], stats[:, 3, :]).then_inc(aggr_done, 1)
                    if late:
                        for j in groups[1:]:
                            rescale(j)

            slots(dve, slot)

        @block.gpsimd
        def _(pool):
            pool.memset(ones[:], 1.0).then_inc(ones_set, 1)
            pool.memset(ctx_nat[:, :, L:L + 1], 1.0).then_inc(ones_set, 1)
            pool.memset(ident[:], 0.0).then_inc(ident_set, 1)
            pool.wait_ge(ident_set, 1)
            pool.affine_select(out=ident[:], in_=ident[:], compare_op=ALU.not_equal, fill=1.0, base=0,
                               pattern=[[-1, P]], channel_multiplier=1).then_inc(ident_set, 1)
            pool.wait_ge(act_bounds, CTX_PARTS)
            pool.wait_ge(dve_bounds, 2)
            pool.partition_all_reduce(max_bound[:, 0:WV], own_bound[:, 0:WV], P, bass.bass_isa.ReduceOp.max)\
                .then_inc(max_bounds, 1)
            pool.wait_ge(dve_bounds, 3)
            pool.partition_all_reduce(max_bound[:, WV:], own_bound[:, WV:], P, bass.bass_isa.ReduceOp.max)\
                .then_inc(max_bounds, 1)
            for q in range(2):
                pool.sem_inc(obuf_free[q], 16)
            pool.wait_ge(constants_set, 3)
            pool.wait_ge(norm_in, 2 * 16)

            def slot(s, k, r):
                share = pool_share(s)
                if is_in(s, 0, B):
                    pool.wait_ge(v_high, s + 1)
                    pool.tensor_tensor(v_part[:, k % 2, LOW], v_scaled[:, k % 2], v_part[:, k % 2, HIGH],
                                       ALU.subtract).then_inc(v_low, 1)
                if is_in(s, 2, B + 2):
                    for j in range(share):
                        pool.wait_ge(norm_done, POOL_J * (s - 2) - moved(s) + j + 1)
                        pool.tensor_tensor(obuf[:, k % 2, j, :], obuf[:, k % 2, j, :], gamma_all[:], ALU.mult)\
                            .then_inc(pool_gamma, 1)
                    pool.wait_ge(pool_gamma, POOL_J * (s - 2) - moved(s) + share)
                    if is_in(s, 2, B + 1):
                        pool.tensor_tensor(obuf[:, k % 2, 0:share, :], obuf[:, k % 2, 0:share, :],
                                           beta_all[:].unsqueeze(1).broadcast_to([P, share, E]), ALU.add)\
                            .then_inc(pool_out, 1)
                    else:
                        for j in range(share):
                            pool.tensor_tensor(obuf[:, k % 2, j, :], obuf[:, k % 2, j, :], beta_all[:], ALU.add)\
                                .then_inc(tail_out[j], 1)
                if is_slot(s, B):
                    for turn, j in enumerate((0, 2)):
                        two = slice(j, j + 2)
                        pool.wait_ge(squares_done, SQUARE_J * (B - 1) + j + 2)
                        pool.tensor_tensor(square_mean[:, two], square_sum[:, two], one_over_e[:, two], ALU.mult)\
                            .then_inc(square_mean_done, 1)
                        pool.wait_ge(square_mean_done, B + turn)
                        pool.tensor_tensor(var_eps[:, two], square_mean[:, two], eps_all[:, two], ALU.add)\
                            .then_inc(var_ready, 1)
                        pool.wait_ge(dve_out, B - 1)
                        pool.wait_ge(var_ready, 2 * (B - 1) + turn + 1)
                        pool.tensor_tensor(rstd[:, two], var_eps[:, two], minus_half[:, two], ALU.pow)\
                            .then_inc(rstd_done, 1)
                        if j == 0:
                            pool.wait_ge(rstd_done, B)
                            pool.tensor_tensor(shift[:, 0:1], neg_mean[:, 0:1], rstd[:, 0:1], ALU.mult)\
                                .then_inc(shift_done, 1)
                elif is_in(s, 1, B + 1):
                    pool.wait_ge(squares_done, SQUARE_J * s)
                    pool.tensor_tensor(square_mean[:, 0:SQUARE_J], square_sum[:, 0:SQUARE_J],
                                       one_over_e[:, 0:SQUARE_J], ALU.mult)\
                        .then_inc(square_mean_done, 1)
                    pool.wait_ge(aggr_done, (RJ - SQUARE_J) * s)
                    pool.tensor_tensor(var_eps[:, SQUARE_J:], mean_var[:, SQUARE_J:, 1], eps_all[:, SQUARE_J:], ALU.add)\
                        .then_inc(var_ready, 1)
                    pool.wait_ge(square_mean_done, s)
                    pool.tensor_tensor(var_eps[:, 0:SQUARE_J], square_mean[:, 0:SQUARE_J], eps_all[:, 0:SQUARE_J], ALU.add)\
                        .then_inc(var_ready, 1)
                    if is_in(s, 2, B + 1):
                        pool.wait_ge(dve_out, s - 1)
                    pool.wait_ge(var_ready, 2 * s)
                    pool.tensor_tensor(rstd[:], var_eps[:], minus_half[:], ALU.pow).then_inc(rstd_done, 1)
                    pool.wait_ge(mean_negated, s)
                    pool.wait_ge(rstd_done, s)
                    pool.tensor_tensor(shift[:], neg_mean[:, 0:POOL_J], rstd[:, 0:POOL_J], ALU.mult).then_inc(shift_done, 1)

            slots(pool, slot)


INPUTS = ["x", "ctx_512", "L0_xattn_Wq", "L0_xattn_bq", "L0_xattn_Wk", "L0_xattn_bk", "L0_xattn_Wv",
          "L0_xattn_bv", "L0_xattn_gamma", "L0_xattn_beta"]


def kernel(**inputs):
    import numpy as np
    import concourse.bacc as bacc
    from concourse.bass_utils import run_bass_kernel_spmd

    nc = bacc.Bacc("TRN2", target_bir_lowering=False, num_devices=1)
    arrays, args = {}, []
    for name in INPUTS:
        a = np.ascontiguousarray(inputs[name])
        arrays[f"in_{name}"] = a
        args.append(nc.dram_tensor(f"in_{name}", a.shape, mybir.dt.from_np(a.dtype), kind="ExternalInput").ap())
    out = nc.dram_tensor("out", arrays["in_x"].shape, F32, kind="ExternalOutput").ap()
    cross_attention(nc, *args, out)
    r = run_bass_kernel_spmd(nc, [arrays], core_ids=[0])
    return r.results[0]["out"]
```

```python
from contextlib import ExitStack

import concourse.bass as bass
from concourse import mybir

P = 128
F32 = mybir.dt.float32
F16 = mybir.dt.float16
I32 = mybir.dt.int32
ALU = mybir.AluOpType
ACT = mybir.ActivationFunctionType
AX = mybir.AxisListType

EPS = 1e-6
RING = 4
LOOP_FROM = 2
POOL_J = 3
LAST_POOL_J = (3, 1, 1)
TAIL = 2
SQUARE_J = 2
PROB_SCALE = 2.0 ** 15
HIGH, LOW = 0, 1
PASSES = ((HIGH, HIGH), (HIGH, LOW), (LOW, HIGH))
EXPONENT_MASK = 0x7F800000
SCALE_FIELD = 127 + 127 + 14
BACK_FIELD = 14
LEAST_BOUND = 2.0 ** -100
CTX_PARTS = 4
WK, WQ, WV = CTX_PARTS, CTX_PARTS + 1, CTX_PARTS + 2


def cross_attention(nc, x, ctx_in, Wq, bq, Wk, bk, Wv, bv, gamma, beta, out):
    B, T, E = x.shape
    _, M, L = ctx_in.shape
    RJ = T // P
    EC = E // P
    FC = Wq.shape[1] // P
    LC = L // P
    SCALE = float(E) ** -0.5
    assert T == RJ * P and E == EC * P and L == LC * P and M <= P and EC * M + 1 <= 512
    assert LAST_POOL_J[-TAIL:] == (1, 1) and TAIL == 2 and B % 2 == 0
    assert LC == 2 and FC == 4 and EC == 4 and B * L <= 2 * RJ * E

    with ExitStack() as stack:
        def sb(name, shape, dt=F32):
            return stack.enter_context(nc.sbuf_tensor(name, shape, dt))

        def bank(name, shape, dt=F32):
            return stack.enter_context(nc.psum_tensor(name, shape, dt))

        def sem(name):
            return stack.enter_context(nc.semaphore(name))

        ident = sb("ident", [P, P])
        wq_nat = sb("wq_nat", [P, EC, E])
        wk_nat = sb("wk_nat", [P, LC, E])
        wqT = sb("wqT", [P, FC, E])
        wkT = sb("wkT", [P, FC, L])
        wv = sb("wv", [P, LC, E])
        wv_part = sb("wv_part", [P, 2, LC, E], F16)
        qk_part = sb("qk_part", [P, 2, LC, E], F16)
        bq_all = sb("bq_all", [P, E])
        bk_all = sb("bk_all", [P, E])
        bv_all = sb("bv_all", [P, E])
        gamma_all = sb("gamma_all", [P, E])
        beta_all = sb("beta_all", [P, E])
        junk = sb("junk", [P, EC + LC + 1, E])
        act_junk = sb("act_junk", [P, B * L + LC * E], F16)
        act_warm = sb("act_warm", [P, RJ])
        u_col = sb("u_col", [P, EC])
        w_col = sb("w_col", [P, LC])
        d_col = sb("d_col", [P, 1])
        ones = sb("ones", [P, M])
        w_diag = sb("w_diag", [P, LC, P])
        w_row = sb("w_row", [M, L + 1])
        key_junk = sb("key_junk", [M, RING, L + 1])
        own_bound = sb("own_bound", [P, 7])
        max_bound = sb("max_bound", [P, 7])
        bv_bound = sb("bv_bound", [P, 1])
        bound = sb("bound", [P, 4])
        field = sb("field", [P, 4])
        scale = sb("scale", [P, 4])
        back = sb("back", [P, 4])
        back_g = sb("back_g", [P, 1])
        back_v = sb("back_v", [P, 1])
        onto_v = sb("onto_v", [P, 1])
        back_y = sb("back_y", [P, 1])
        bv_scaled = sb("bv_scaled", [P, E])
        ctx_nat = sb("ctx_nat", [M, RING, L + 1])
        ctxT = sb("ctxT", [P, 2, 2, LC, M], F16)
        xbuf = sb("xbuf", [P, RING, RJ, E])
        obuf = sb("obuf", [P, 2, RJ, E])
        xT = sb("xT", [P, EC, T])
        gT = sb("gT", [P, 2, EC, M])
        c_key = sb("c_key", [M, RING, 1])
        probs = sb("probs", [M, T])
        prob_part = sb("prob_part", [M, 2, T], F16)
        v_scaled = sb("v_scaled", [M, 2, E])
        v_part = sb("v_part", [M, 2, 2, E], F16)
        s_max = sb("s_max", [M, 1])
        s_neg = sb("s_neg", [M, 1])
        s_bias = sb("s_bias", [M, 1])
        s_sum = sb("s_sum", [M, 1])
        s_rec = sb("s_rec", [M, 1])
        s_by = sb("s_by", [M, 1])
        stats = sb("stats", [P, RJ, 6])
        mean_var = sb("mean_var", [P, RJ, 2])
        square_junk = sb("square_junk", [P, RJ, E])
        y_sum = sb("y_sum", [P, RJ])
        square_sum = sb("square_sum", [P, RJ])
        square_mean = sb("square_mean", [P, RJ])
        one_over_e = sb("one_over_e", [P, RJ])
        eps_all = sb("eps_all", [P, RJ])
        minus_half = sb("minus_half", [P, RJ])
        var_eps = sb("var_eps", [P, RJ])
        neg_mean = sb("neg_mean", [P, 2, RJ])
        rstd = sb("rstd", [P, 2, RJ])
        shift = sb("shift", [P, POOL_J])

        xT_ps = [bank(f"xT_ps{i}", [P, RJ, P]) for i in range(2)]
        ctx_ps = bank("ctx_ps", [P, 512])
        v_ps = bank("v_ps", [P, 512])
        g_ps = bank("g_ps", [P, 512])
        s_ps = bank("s_ps", [P, 512])
        pv_ps = [bank(f"pv_ps{i}", [P, 512]) for i in range(2)]
        y_ps = [bank_[:] for bank_ in (pv_ps[0], pv_ps[1], v_ps, pv_ps[0])]
        last_y_ps = [*(bank_[:].rearrange("p j q -> p (j q)") for bank_ in xT_ps), ctx_ps[:], g_ps[:]]
        ctxT_v = ctx_ps[:, 0:LC * M].rearrange("p (c m) -> p c m", m=M)
        g_v = g_ps[:, 0:EC * M].rearrange("p (c m) -> p c m", m=M)
        w_ps = v_ps[0:M, 0:L]
        ctx_all = obuf[0:M].rearrange("m q j e -> m (q j e)")[:, 0:B * L]

        ident_set = sem("ident_set")
        bound_cleared = sem("bound_cleared")
        wk_in = sem("wk_in")
        wq_in = [sem(f"wq_in{h}") for h in range(2)]
        wv_in = sem("wv_in")
        ctx_all_in = [sem(f"ctx_all_in{h}") for h in range(2)]
        bqk_in = sem("bqk_in")
        bv_in = sem("bv_in")
        norm_in = sem("norm_in")
        ctx_loaded = [sem(f"ctx_loaded{k}") for k in range(RING)]
        x_in = [sem(f"x_in{k}") for k in range(RING)]
        obuf_free = [sem(f"obuf_free{q}") for q in range(2)]
        wT_turned = sem("wT_turned")
        wT_copied = sem("wT_copied")
        qk_done = sem("qk_done")
        act_bounds = sem("act_bounds")
        dve_bounds = sem("dve_bounds")
        max_bounds = sem("max_bounds")
        scales_step = sem("scales_step")
        scales_done = sem("scales_done")
        back_done = sem("back_done")
        high_split = sem("high_split")
        low_split = sem("low_split")
        dots_done = sem("dots_done")
        ones_set = sem("ones_set")
        w_diag_done = sem("w_diag_done")
        w_spread = sem("w_spread")
        w_row_done = sem("w_row_done")
        key_done = sem("key_done")
        constants_set = sem("constants_set")
        xT_turned = sem("xT_turned")
        xT_copied = sem("xT_copied")
        ctx_turned = sem("ctx_turned")
        ctx_high = sem("ctx_high")
        ctx_low = sem("ctx_low")
        v_done = sem("v_done")
        v_copied = sem("v_copied")
        g_done = sem("g_done")
        g_copied = sem("g_copied")
        scores_done = sem("scores_done")
        max_done = sem("max_done")
        neg_done = sem("neg_done")
        bias_done = sem("bias_done")
        probs_done = sem("probs_done")
        rec_done = sem("rec_done")
        by_done = sem("by_done")
        prob_high = sem("prob_high")
        prob_low = sem("prob_low")
        v_high = sem("v_high")
        v_low = sem("v_low")
        pv_done = sem("pv_done")
        y_done = sem("y_done")
        stats_done = sem("stats_done")
        aggr_done = sem("aggr_done")
        var_ready = sem("var_ready")
        sums_negated = sem("sums_negated")
        mean_negated = sem("mean_negated")
        squares_done = sem("squares_done")
        square_mean_done = sem("square_mean_done")
        rstd_done = sem("rstd_done")
        shift_done = sem("shift_done")
        norm_done = sem("norm_done")
        pool_gamma = sem("pool_gamma")
        pool_out = sem("pool_out")
        dve_gamma = sem("dve_gamma")
        dve_out = sem("dve_out")
        tail_out = [[sem(f"tail_out{b}_{j}") for j in range(RJ)] for b in range(TAIL)]
        tail_stored = sem("tail_stored")

        def slots(eng, slot, loop_from=LOOP_FROM, end=B + 2):
            loop_to = loop_from + (B - 2 - loop_from) // RING * RING
            for s in range(loop_from):
                slot(s, s % RING, s // RING)
            with eng.Fori(0, (loop_to - loop_from) // RING) as turn:
                for i in range(loop_from, loop_from + RING):
                    slot(turn * RING + i, i % RING, turn + i // RING)
            for s in range(loop_to, end):
                slot(s, s % RING, s // RING)

        def is_in(s, low, high):
            return low <= s < high if isinstance(s, int) else True

        def obuf_fills(k, r):
            return 16 * (r * (RING // 2) + (k - 2) // 2 + 1)

        def is_slot(s, which):
            return isinstance(s, int) and s == which

        def pool_share(s):
            return LAST_POOL_J[s - B + 1] if isinstance(s, int) and s >= B - 1 else POOL_J

        def moved(s):
            return sum(POOL_J - share for share in LAST_POOL_J[:s - B + 1]) if isinstance(s, int) and s >= B else 0

        block = stack.enter_context(nc.Block())

        @block.sync
        def _(sp):
            def load_x(b, k):
                sp.dma_start(xbuf[:, k], x[bass.ds(b, 1)].rearrange("o (p j) e -> p (o j) e", j=RJ))\
                    .then_inc(x_in[k], 16)

            def load_ctx(b, k):
                sp.dma_start(ctx_nat[:, k, 0:L], ctx_in[bass.ds(b, 1)].rearrange("o m l -> m (o l)"))\
                    .then_inc(ctx_loaded[k], 16)

            sp.dma_start(wk_nat[:], Wk.rearrange("(c p) f -> p c f", p=P)).then_inc(wk_in, 16)
            for h in range(2):
                f = slice(h * E // 2, (h + 1) * E // 2)
                sp.dma_start(wq_nat[:, :, f], Wq.rearrange("(c p) f -> p c f", p=P)[:, :, f]).then_inc(wq_in[h], 16)
            load_ctx(0, 0)
            all_v = ctx_all.rearrange("m (b l) -> m b l", l=L)
            for h in range(2):
                sp.dma_start(all_v[:, h * B // 2:(h + 1) * B // 2],
                             ctx_in[h * B // 2:(h + 1) * B // 2].rearrange("b m l -> m b l"))\
                    .then_inc(ctx_all_in[h], 16)
            load_x(0, 0)
            sp.dma_start(wv[:], Wv.rearrange("(c p) e -> p c e", p=P)).then_inc(wv_in, 16)
            load_ctx(1, 1)
            sp.dma_start(bv_all[:], bv.partition_broadcast(P)).then_inc(bv_in, 16)

            def slot(s, k, r):
                if is_in(s, 2, B - 2):
                    sp.wait_ge(ctx_turned, s - 1)
                    sp.wait_ge(key_done, s - 1)
                if is_in(s, 0, B - 2):
                    load_ctx(s + 2, (k + 2) % RING)
                if is_in(s, 3, B - 1):
                    sp.wait_ge(norm_done, POOL_J * (s - 2))
                    sp.wait_ge(dve_gamma, (RJ - POOL_J) * (s - 2))
                if is_in(s, 0, B - 1):
                    load_x(s + 1, (k + 1) % RING)
                if is_slot(s, 0):
                    sp.dma_start(gamma_all[:], gamma.partition_broadcast(P)).then_inc(norm_in, 16)
                    sp.dma_start(beta_all[:], beta.partition_broadcast(P)).then_inc(norm_in, 16)
                if is_in(s, 3, B + 3 - TAIL):
                    sp.wait_ge(pool_out, s - 2)
                    sp.wait_ge(dve_out, s - 2)
                    sp.dma_start(out[bass.ds(s - 3, 1)].rearrange("o (p j) e -> p (o j) e", j=RJ),
                                 obuf[:, (k + 1) % 2]).then_inc(obuf_free[(k + 1) % 2], 16)

            slots(sp, slot, loop_from=3, end=B + 3 - TAIL)
            for b in range(B - TAIL, B):
                share = pool_share(b + 2)
                for j in (*range(share, RJ), *range(share)):
                    sp.wait_ge(tail_out[b - B + TAIL][j], 1)
                    sp.dma_start(out[b].rearrange("(p j) e -> p j e", j=RJ)[:, j], obuf[:, b % 2, j])\
                        .then_inc(tail_stored, 16)
            for q in range(2):
                sp.wait_ge(obuf_free[q], 16 * ((B - TAIL) // 2 + 1))
            sp.wait_ge(tail_stored, 16 * TAIL * RJ)

        @block.tensor
        def _(pe):
            def keep_warm(n, ps):
                for _ in range(n):
                    pe.transpose(ps[:, 0:P], ident[:], ident[:])

            pe.wait_ge(ident_set, 2)
            keep_warm(12, g_ps)
            pe.wait_ge(wk_in, 16)
            for h, ps in enumerate((ctx_ps, v_ps)):
                for f in range(2 * h, 2 * h + 2):
                    for c in range(LC):
                        col = (f - 2 * h) * L + c * P
                        mm = pe.transpose(ps[:, col:col + P], wk_nat[:, c, f * P:(f + 1) * P], ident[:])
                mm.then_inc(wT_turned, 1)
            keep_warm(3, g_ps)
            pe.wait_ge(wq_in[0], 16)
            qk_ps = (g_ps, s_ps)

            def turn_wq(f):
                if f >= 2:
                    pe.wait_ge(wT_copied, 2 + f - 1)
                for c in range(EC):
                    mm = pe.transpose(xT_ps[f % 2][:, c, :], wq_nat[:, c, f * P:(f + 1) * P], ident[:])
                mm.then_inc(wT_turned, 1)

            def multiply_qk(f):
                pe.wait_ge(wT_copied, 2 + f + 1)
                for c in range(LC):
                    mm = pe.matmul(qk_ps[c][:], wkT[:, f, c * P:(c + 1) * P], wqT[:, f, :],
                                   start=(f == 0), stop=(f == FC - 1))
                    if f == FC - 1:
                        mm.then_inc(qk_done, 1)

            def turn_ctx(b, k, r):
                if is_in(b, 1, B):
                    pe.wait_ge(ctx_low, b)
                pe.wait_ge(ctx_loaded[k], 16 * (r + 1))
                for c in range(LC):
                    mm = pe.transpose(ctxT_v[:, c, :], ctx_nat[:, k, c * P:(c + 1) * P], ident[0:M, 0:M])
                mm.then_inc(ctx_turned, 1)

            def context_v(b, k):
                pe.wait_ge(ctx_low, b + 1)
                if is_in(b, 1, B):
                    pe.wait_ge(v_copied, b)
                if is_in(b, 3, B):
                    pe.wait_ge(y_done, RJ * (b - 3) + 3)
                steps = [(c, *parts) for c in range(LC) for parts in PASSES]
                for n, (c, of_ctx, of_w) in enumerate(steps):
                    mm = pe.matmul(v_ps[0:M, :], ctxT[:, k % 2, of_ctx, c, :], wv_part[:, of_w, c, :],
                                   start=(n == 0), stop=(n == len(steps) - 1))
                mm.then_inc(v_done, 1)

            def context_g(b, k):
                pe.wait_ge(ctx_low, b + 1)
                if is_in(b, 1, B):
                    pe.wait_ge(g_copied, EC * b)
                steps = [(c, *parts) for c in range(LC) for parts in PASSES]
                for e in range(EC):
                    for n, (c, of_w, of_ctx) in enumerate(steps):
                        mm = pe.matmul(g_v[:, e, :], qk_part[:, of_w, c, e * P:(e + 1) * P],
                                       ctxT[:, k % 2, of_ctx, c, :], start=(n == 0), stop=(n == len(steps) - 1))
                mm.then_inc(g_done, 1)

            def turn_x(s, k, e):
                if is_in(s, 1, B) or e >= 2:
                    pe.wait_ge(xT_copied, EC * s + e - 1)
                for j in range(RJ):
                    mm = pe.transpose(xT_ps[e % 2][:, j, :], xbuf[:, k, j, e * P:(e + 1) * P], ident[:])
                mm.then_inc(xT_turned, 1)

            def product(b, k, j):
                banks = last_y_ps if is_slot(b, B - 1) else y_ps
                if j == 0 and is_in(b, 1, B - 1):
                    pe.wait_ge(y_done, RJ * b)
                if j == 2 and is_in(b, 0, B - 2):
                    pe.wait_ge(v_copied, b + 3)
                if j == 3 and is_in(b, 0, B - 1):
                    pe.wait_ge(y_done, RJ * b + 1)
                for n, (of_p, of_v) in enumerate(PASSES):
                    if j == 0 and n == len(PASSES) - 1:
                        pe.wait_ge(prob_low, b + 1)
                    mm = pe.matmul(banks[j], prob_part[:, of_p, j * P:(j + 1) * P], v_part[:, k % 2, of_v, :],
                                   start=(n == 0), stop=(n == len(PASSES) - 1))
                mm.then_inc(pv_done, 1)

            def scores(s, k):
                for e in range(EC):
                    pe.wait_ge(g_copied, EC * s + e + 1)
                    pe.wait_ge(xT_copied, EC * s + e + 1)
                    mm = pe.matmul(s_ps[0:M, :], gT[:, k % 2, e, :], xT[:, e, :],
                                   start=(e == 0), stop=(e == EC - 1))
                mm.then_inc(scores_done, 1)

            turn_wq(0)
            turn_wq(1)
            multiply_qk(0)
            pe.wait_ge(wq_in[1], 16)
            turn_wq(2)
            multiply_qk(1)
            pe.wait_ge(wT_copied, 1)
            turn_ctx(0, 0, 0)
            turn_wq(3)
            pe.wait_ge(wT_copied, 2)
            pe.wait_ge(ones_set, 1)
            pe.wait_ge(w_diag_done, LC)
            for c in range(LC):
                mm = pe.matmul(w_ps[:, c * P:(c + 1) * P], ones[:], w_diag[:, c, :], start=True, stop=True)
            mm.then_inc(w_spread, 1)
            multiply_qk(2)
            multiply_qk(3)
            keep_warm(9, pv_ps[0])
            pe.wait_ge(wT_copied, 2 + FC)
            pe.wait_ge(x_in[0], 16)
            turn_x(0, 0, 0)
            turn_x(0, 0, 1)
            pe.wait_ge(high_split, 2)
            pe.wait_ge(low_split, 2)
            context_g(0, 0)
            turn_x(0, 0, 2)
            turn_x(0, 0, 3)
            turn_ctx(1, 1, 0)
            scores(0, 0)
            context_g(1, 1)
            pe.wait_ge(high_split, 3)
            pe.wait_ge(low_split, 3)
            context_v(0, 0)
            turn_ctx(2, 2, 0)

            def slot(s, k, r):
                if is_slot(s, 0):
                    return
                main, last = is_in(s, 0, B), is_in(s, 1, B + 1)
                more = is_in(s, 0, B - 1)
                k1 = (k + 1) % RING
                if main:
                    pe.wait_ge(x_in[k], 16 * (r + 1))
                    turn_x(s, k, 0)
                    turn_x(s, k, 1)
                if is_slot(s, 1):
                    context_v(1, 1)
                elif more:
                    context_v(s + 1, k1)
                if main:
                    turn_x(s, k, 2)
                    turn_x(s, k, 3)
                if more:
                    context_g(s + 1, k1)
                if is_slot(s, 1):
                    context_v(2, 2)
                if is_slot(s, B - 1):
                    pe.wait_ge(probs_done, s)
                    scores(s, k)
                if is_slot(s, B):
                    keep_warm(12, g_ps)
                if last:
                    pe.wait_ge(v_low, s)
                    pe.wait_ge(prob_high, s)
                    product(s - 1, k + 1, 0)
                    product(s - 1, k + 1, 1)
                    product(s - 1, k + 1, 2)
                if is_in(s, 0, B - 2):
                    turn_ctx(s + 2, (k + 2) % RING, r + (k + 2) // RING)
                if last:
                    product(s - 1, k + 1, 3)
                if main and not is_slot(s, B - 1):
                    scores(s, k)

            slots(pe, slot)

        @block.scalar
        def _(act):
            act.dma_start(bq_all[:], bq.partition_broadcast(P)).then_inc(bqk_in, 16)
            act.dma_start(bk_all[:], bk.partition_broadcast(P)).then_inc(bqk_in, 16)
            act.wait_ge(constants_set, 3)
            act.activation(act_warm[:], eps_all[:], ACT.Copy)
            act.wait_ge(wT_turned, 1)
            act.activation(wkT[:, 0:2, :], ctx_ps[:].rearrange("p (f l) -> p f l", l=L), ACT.Copy)\
                .then_inc(wT_copied, 1)
            act.wait_ge(wT_turned, 2)
            act.activation(wkT[:, 2:4, :], v_ps[:].rearrange("p (f l) -> p f l", l=L), ACT.Copy)\
                .then_inc(wT_copied, 1)
            act.wait_ge(bound_cleared, 1)
            act.activation(act_junk[:, B * L:B * L + LC * E].rearrange("p (c e) -> p c e", e=E), wk_nat[:], ACT.Abs,
                           accum_out=own_bound[:, WK:WK + 1]).then_inc(act_bounds, 1)
            part = B * L // CTX_PARTS

            def copy_wqT(f):
                act.wait_ge(wT_turned, 3 + f)
                act.activation(wqT[:, f, :].rearrange("p (c q) -> p c q", q=P), xT_ps[f % 2][:], ACT.Copy)\
                    .then_inc(wT_copied, 1)

            def sum_ctx(h):
                act.wait_ge(ctx_all_in[h * 2 // CTX_PARTS], 16)
                act.activation(act_junk[0:M, h * part:(h + 1) * part], ctx_all[:, h * part:(h + 1) * part], ACT.Abs,
                               accum_out=own_bound[0:M, h:h + 1]).then_inc(act_bounds, 1)

            copy_wqT(0)
            copy_wqT(1)
            sum_ctx(0)
            copy_wqT(2)
            sum_ctx(1)
            copy_wqT(3)
            sum_ctx(2)
            act.wait_ge(scales_done, 1)
            def ctx_to_high(b, k):
                act.wait_ge(ctx_turned, b + 1)
                if is_in(b, 2, B):
                    act.wait_ge(g_done, b - 1)
                act.activation(ctxT[:, k % 2, HIGH], ctxT_v, ACT.Copy, scale=scale[:, 0:1]).then_inc(ctx_high, 1)

            def copy_xT(s, e):
                act.wait_ge(xT_turned, EC * s + e + 1)
                act.activation(xT[:, e, :].rearrange("p (j q) -> p j q", q=P), xT_ps[e % 2][:], ACT.Copy)\
                    .then_inc(xT_copied, 1)

            def copy_g(b, k):
                act.wait_ge(g_done, b + 1)
                for e in range(EC):
                    act.activation(gT[:, k % 2, e, :], g_v[:, e, :], ACT.Identity, scale=back_g[:],
                                   bias=u_col[:, e:e + 1]).then_inc(g_copied, 1)

            ctx_to_high(0, 0)
            for c in range(LC):
                act.wait_ge(qk_done, c + 1)
                act.activation(qk_part[:, HIGH, c, :], (g_ps, s_ps)[c][:], ACT.Copy, scale=scale[:, 1:2])\
                    .then_inc(high_split, 1)
            copy_xT(0, 0)
            copy_xT(0, 1)
            act.wait_ge(back_done, 1)
            act.wait_ge(dots_done, LC + 1 + EC)
            copy_g(0, 0)
            copy_xT(0, 2)
            copy_xT(0, 3)
            ctx_to_high(1, 1)
            act.wait_ge(scales_done, 2)
            act.activation(wv_part[:, HIGH], wv[:], ACT.Copy, scale=scale[:, 2:3]).then_inc(high_split, 1)

            def slot(s, k, r):
                kb, kn = (k - 1) % RING, (k - 2) % RING
                main = is_in(s, 1, B)

                def v_to_high(b, parity):
                    act.wait_ge(v_copied, b + 1)
                    if is_in(b, 2, B):
                        act.wait_ge(pv_done, RJ * (b - 1))
                    act.activation(v_part[:, parity, HIGH], v_scaled[:, parity], ACT.Copy).then_inc(v_high, 1)

                if is_in(s, 2, B):
                    v_to_high(s, k % 2)
                if main:
                    copy_xT(s, 0)
                    copy_xT(s, 1)

                def exponential(b):
                    act.wait_ge(bias_done, b + 1)
                    act.activation(probs[:], s_ps[0:M, :], ACT.Exp, bias=s_bias[:], scale=SCALE,
                                   accum_out=s_sum[:]).then_inc(probs_done, 1)

                def probs_to_high(b):
                    act.wait_ge(by_done, b + 1)
                    act.activation(prob_part[:, HIGH], probs[:], ACT.Copy, scale=s_by[:]).then_inc(prob_high, 1)

                def square(j):
                    act.activation(square_junk[:, j], xbuf[:, kb, j, :], ACT.Square,
                                   bias=neg_mean[:, (k + 1) % 2, j:j + 1], accum_out=square_sum[:, j:j + 1])\
                        .then_inc(squares_done, 1)

                def normalise():
                    act.wait_ge(shift_done, s - 1)
                    act.wait_ge(obuf_free[k % 2], obuf_fills(k, r))
                    for j in range(pool_share(s)):
                        act.activation(obuf[:, k % 2, j, :], xbuf[:, kn, j, :], ACT.Identity,
                                       bias=shift[:, j:j + 1], scale=rstd[:, k % 2, j:j + 1]).then_inc(norm_done, 1)

                if is_in(s, 1, B):
                    exponential(s - 1)
                    if is_slot(s, 1):
                        ctx_to_high(2, 2)
                    probs_to_high(s - 1)
                if is_slot(s, 1):
                    v_to_high(0, 0)
                if is_slot(s, B - 1):
                    copy_xT(s, 2)
                    copy_xT(s, 3)
                if is_in(s, 2, B) or is_slot(s, B + 1):
                    normalise()
                if main and not is_slot(s, B - 1):
                    copy_xT(s, 2)
                    copy_xT(s, 3)
                if is_slot(s, 1):
                    v_to_high(1, 1)
                if is_in(s, 1, B - 2):
                    ctx_to_high(s + 2, k + 2)
                if is_in(s, 0, B - 1):
                    copy_g(s + 1, k + 1)
                if is_slot(s, B - 1):
                    exponential(s)
                    act.wait_ge(pv_done, RJ * s)
                    probs_to_high(s)
                    for j in range(RJ):
                        act.wait_ge(sums_negated, s + j // 2)
                        square(j)
                elif is_slot(s, B):
                    act.wait_ge(square_mean_done, s - 1)
                    for j in range(RJ):
                        act.wait_ge(sums_negated, s + 1 + j)
                        square(j)
                        if j == 1:
                            normalise()
                elif is_in(s, 1, B - 1):
                    act.wait_ge(sums_negated, s)
                    for j in range(SQUARE_J):
                        square(j)

            slots(act, slot)

        @block.vector
        def _(dve):
            dve.memset(own_bound[:], 0.0).then_inc(bound_cleared, 1)
            dve.memset(minus_half[:], -0.5).then_inc(constants_set, 1)
            dve.memset(eps_all[:], EPS).then_inc(constants_set, 1)
            dve.memset(one_over_e[:], 1.0 / E).then_inc(constants_set, 1)

            def largest(out_, in_):
                dve.tensor_reduce(out_, in_, AX.X, ALU.max, apply_absolute_value=True).then_inc(dve_bounds, 1)

            def dot(n, in_, bias_row, out_):
                dve.scalar_tensor_tensor(junk[:, n], in_, 1.0, bias_row[:], ALU.mult, ALU.mult, accum_out=out_)\
                    .then_inc(dots_done, 1)

            dve.wait_ge(bqk_in, 2 * 16)
            dot(LC + EC, bk_all[:], bq_all, d_col[:])
            dve.wait_ge(wk_in, 16)
            for c in range(LC):
                dot(c, wk_nat[:, c], bq_all, w_col[:, c:c + 1])
            dve.wait_ge(ident_set, 2)
            dve.wait_ge(dots_done, LC + 1)
            for c in range(LC):
                dve.tensor_scalar(w_diag[:, c, :], ident[:], w_col[:, c:c + 1], None, ALU.mult)\
                    .then_inc(w_diag_done, 1)
            dve.tensor_copy(w_row[:, L:L + 1], d_col[0:M, :])
            dve.wait_ge(wq_in[0], 16)
            dve.wait_ge(wq_in[1], 16)
            dve.wait_ge(bound_cleared, 1)
            largest(own_bound[:, WQ:WQ + 1], wq_nat[:].rearrange("p c e -> p (c e)"))
            for c in range(EC):
                dot(LC + c, wq_nat[:, c], bk_all, u_col[:, c:c + 1])
            dve.wait_ge(ctx_all_in[1], 16)
            dve.tensor_reduce(own_bound[0:M, CTX_PARTS - 1:CTX_PARTS],
                              ctx_all[:, (CTX_PARTS - 1) * B * L // CTX_PARTS:], AX.X, ALU.add,
                              apply_absolute_value=True).then_inc(dve_bounds, 1)
            dve.wait_ge(w_spread, 1)
            dve.tensor_copy(w_row[:, 0:L], w_ps).then_inc(w_row_done, 1)
            step = 0

            def scales(instruction):
                nonlocal step
                step += 1
                instruction.then_inc(scales_step, 1)
                dve.wait_ge(scales_step, step)

            def exact_scales(low, high):
                scales(dve.tensor_scalar(bound[:, low:high], bound[:, low:high], LEAST_BOUND, None, ALU.max))
                scales(dve.tensor_scalar(field[:, low:high].bitcast(I32), bound[:, low:high].bitcast(I32),
                                         EXPONENT_MASK, None, ALU.bitwise_and))
                dve.tensor_scalar(scale[:, low:high].bitcast(I32), field[:, low:high].bitcast(I32), -1.0,
                                  float(SCALE_FIELD << 23), ALU.mult, ALU.add).then_inc(scales_done, 1)
                scales(dve.tensor_scalar(back[:, low:high].bitcast(I32), field[:, low:high].bitcast(I32),
                                         float(BACK_FIELD << 23), None, ALU.subtract))

            dve.wait_ge(max_bounds, 1)
            dve.tensor_reduce(bound[:, 0:1], max_bound[:, 0:CTX_PARTS], AX.X, ALU.max)
            scales(dve.tensor_tensor(bound[:, 1:2], max_bound[:, WQ:WQ + 1], max_bound[:, WK:WK + 1], ALU.mult))
            exact_scales(0, 2)
            dve.tensor_tensor(back_g[:], back[:, 0:1], back[:, 1:2], ALU.mult).then_inc(back_done, 1)
            dve.wait_ge(scales_done, 1)

            def low_part(out_, in_, by, high, n):
                dve.wait_ge(high_split, n)
                dve.scalar_tensor_tensor(out_, in_, by, high, ALU.mult, ALU.subtract).then_inc(low_split, 1)

            def ctx_to_low(b, k):
                dve.wait_ge(ctx_high, b + 1)
                dve.scalar_tensor_tensor(ctxT[:, k % 2, LOW], ctxT_v, scale[:, 0:1], ctxT[:, k % 2, HIGH],
                                         ALU.mult, ALU.subtract).then_inc(ctx_low, 1)

            ctx_to_low(0, 0)
            low_part(qk_part[:, LOW, 0, :], g_ps[:], scale[:, 1:2], qk_part[:, HIGH, 0, :], 1)
            low_part(qk_part[:, LOW, 1, :], s_ps[:], scale[:, 1:2], qk_part[:, HIGH, 1, :], 2)
            dve.wait_ge(wv_in, 16)
            largest(own_bound[:, WV:WV + 1], wv[:].rearrange("p c e -> p (c e)"))
            dve.wait_ge(bv_in, 16)
            largest(bv_bound[:], bv_all[:])
            dve.wait_ge(max_bounds, 2)
            dve.tensor_copy(bound[:, 2:3], max_bound[:, WV:WV + 1])
            dve.wait_ge(dve_bounds, 4)
            scales(dve.scalar_tensor_tensor(bound[:, 3:4], bound[:, 0:1], max_bound[:, WV:WV + 1], bv_bound[:],
                                            ALU.mult, ALU.add))
            exact_scales(2, 4)
            dve.wait_ge(scales_done, 2)
            dve.tensor_scalar(back_y[:], back[:, 3:4], 1.0 / PROB_SCALE, None, ALU.mult)
            dve.tensor_scalar(bv_scaled[:], bv_all[:], scale[:, 3:4], None, ALU.mult)
            scales(dve.tensor_tensor(back_v[:], back[:, 0:1], back[:, 2:3], ALU.mult))
            ctx_to_low(1, 1)
            dve.tensor_tensor(onto_v[:], back_v[:], scale[:, 3:4], ALU.mult)
            low_part(wv_part[:, LOW], wv[:], scale[:, 2:3], wv_part[:, HIGH], 3)
            dve.wait_ge(low_split, 3)

            def key_bias(b, k, r):
                dve.wait_ge(ctx_loaded[k], 16 * (r + 1))
                dve.scalar_tensor_tensor(key_junk[:, k], ctx_nat[:, k], 1.0, w_row[:], ALU.mult, ALU.mult,
                                         accum_out=c_key[:, k]).then_inc(key_done, 1)

            dve.wait_ge(w_row_done, 1)
            dve.wait_ge(ones_set, 2)
            key_bias(0, 0, 0)
            key_bias(1, 1, 0)

            def copy_v(b, k):
                dve.wait_ge(v_done, b + 1)
                if is_in(b, 2, B):
                    dve.wait_ge(v_low, b - 1)
                dve.scalar_tensor_tensor(v_scaled[:, k % 2], v_ps[0:M, :], onto_v[0:M, :], bv_scaled[0:M, :],
                                         ALU.mult, ALU.add).then_inc(v_copied, 1)


            def slot(s, k, r):
                kb, kn = (k - 1) % RING, (k - 2) % RING
                groups = range(pool_share(s), RJ)

                def softmax_bias(b, kb):
                    dve.wait_ge(key_done, b + 1)
                    dve.wait_ge(scores_done, b + 1)
                    dve.tensor_reduce(s_max[:], s_ps[0:M, :], AX.X, ALU.max).then_inc(max_done, 1)
                    dve.wait_ge(max_done, b + 1)
                    dve.tensor_scalar(s_neg[:], s_max[:], c_key[:, kb], -SCALE, ALU.add, ALU.mult)\
                        .then_inc(neg_done, 1)
                    dve.wait_ge(neg_done, b + 1)
                    dve.tensor_scalar(s_bias[:], c_key[:, kb], SCALE, s_neg[:], ALU.mult, ALU.add)\
                        .then_inc(bias_done, 1)

                def softmax_scale(b):
                    dve.wait_ge(probs_done, b + 1)
                    dve.reciprocal(s_rec[:], s_sum[:]).then_inc(rec_done, 1)
                    dve.wait_ge(rec_done, b + 1)
                    dve.tensor_scalar(s_by[:], s_rec[:], PROB_SCALE, None, ALU.mult).then_inc(by_done, 1)

                def probs_to_low(b):
                    dve.wait_ge(prob_high, b + 1)
                    dve.scalar_tensor_tensor(prob_part[:, LOW], probs[:], s_by[:], prob_part[:, HIGH],
                                             ALU.mult, ALU.subtract).then_inc(prob_low, 1)

                def center(j):
                    by, op = neg_mean[:, k % 2, j:j + 1], ALU.add
                    if is_in(s, 2, B):
                        dve.wait_ge(aggr_done, (RJ - SQUARE_J) * (s - 1))
                        dve.wait_ge(mean_negated, s - 1)
                        if j == RJ - 1:
                            by, op = mean_var[:, j, 0:1], ALU.subtract
                    else:
                        dve.wait_ge(sums_negated, B if s == B else B + RJ)
                    dve.wait_ge(obuf_free[k % 2], obuf_fills(k, r))
                    dve.scalar_tensor_tensor(obuf[:, k % 2, j, :], xbuf[:, kn, j, :], by, gamma_all[:], op, ALU.mult)\
                        .then_inc(dve_gamma, 1)

                def rescale(j):
                    dve.wait_ge(rstd_done, s - 1)
                    dve.wait_ge(dve_gamma, (RJ - POOL_J) * (s - 2) + moved(s) + j - groups[0] + 1)
                    done = dve.scalar_tensor_tensor(obuf[:, k % 2, j, :], obuf[:, k % 2, j, :],
                                                    rstd[:, k % 2, j:j + 1], beta_all[:], ALU.mult, ALU.add)
                    if is_slot(s, B) or is_slot(s, B + 1):
                        done.then_inc(tail_out[s - B][j], 1)
                    elif j == RJ - 1:
                        done.then_inc(dve_out, 1)

                def residual(j):
                    sum_too = j < SQUARE_J or not is_in(s, 1, B - 1)
                    dve.wait_ge(pv_done, RJ * (s - 1) + j + 1)
                    dve.scalar_tensor_tensor(xbuf[:, kb, j, :], (last_y_ps if is_slot(s, B) else y_ps)[j], back_y[:],
                                             xbuf[:, kb, j, :], ALU.mult, ALU.add,
                                             accum_out=y_sum[:, j:j + 1] if sum_too else None).then_inc(y_done, 1)

                def negate(low, high):
                    dve.wait_ge(y_done, RJ * (s - 1) + high)
                    dve.tensor_scalar(neg_mean[:, (k + 1) % 2, low:high], y_sum[:, low:high], -1.0 / E, None,
                                      ALU.mult).then_inc(sums_negated, 1)

                def statistics(j):
                    dve.wait_ge(y_done, RJ * (s - 1) + j + 1)
                    dve.bn_stats(stats[:, j, :], xbuf[:, kb, j, :]).then_inc(stats_done, 1)

                if is_in(s, 1, B):
                    softmax_bias(s - 1, (k - 1) % RING)
                if is_in(s, 2, B):
                    for j in groups:
                        center(j)
                if is_slot(s, 1):
                    copy_v(0, 0)
                if is_in(s, 1, B):
                    softmax_scale(s - 1)
                if is_slot(s, 1):
                    ctx_to_low(2, 2)
                    copy_v(1, 1)
                    dve.wait_ge(norm_in, 2 * 16)
                if is_in(s, 2, B - 1):
                    copy_v(s + 1, k + 1)
                if is_in(s, 1, B):
                    probs_to_low(s - 1)
                if is_slot(s, 1):
                    copy_v(2, 2)
                if is_in(s, 2, B):
                    for j in groups:
                        rescale(j)
                if is_in(s, 1, B - 1):
                    if is_in(s, 2, B):
                        dve.wait_ge(shift_done, s - 1)
                    residual(0)
                    residual(1)
                if is_in(s, 1, B - 2):
                    ctx_to_low(s + 2, k + 2)
                if is_in(s, 0, B - 2):
                    key_bias(s + 2, (k + 2) % RING, r + (k + 2) // RING)
                if is_in(s, 1, B - 1):
                    residual(2)
                    negate(0, SQUARE_J)
                    residual(3)
                    statistics(2)
                    dve.wait_ge(stats_done, (RJ - SQUARE_J) * (s - 1) + 1)
                    statistics(3)
                    dve.bn_aggr(mean_var[:, 2, :], stats[:, 2, :]).then_inc(aggr_done, 1)
                    dve.wait_ge(stats_done, (RJ - SQUARE_J) * s)
                    dve.wait_ge(aggr_done, (RJ - SQUARE_J) * s - 1)
                    dve.tensor_scalar(neg_mean[:, (k + 1) % 2, 2:3], mean_var[:, 2:3, 0], -1.0, None, ALU.mult)\
                        .then_inc(mean_negated, 1)
                    dve.bn_aggr(mean_var[:, 3, :], stats[:, 3, :]).then_inc(aggr_done, 1)
                elif is_slot(s, B - 1):
                    softmax_bias(s, k)
                    residual(0)
                    softmax_scale(s)
                    residual(1)
                    residual(2)
                    negate(0, 2)
                    probs_to_low(s)
                    residual(3)
                    negate(2, 4)
                elif is_slot(s, B):
                    residual(0)
                    residual(1)
                    negate(0, 1)
                    residual(2)
                    negate(1, 2)
                    residual(3)
                    negate(2, 3)
                    negate(3, 4)
                if is_slot(s, B) or is_slot(s, B + 1):
                    for j in groups:
                        center(j)
                    for j in groups:
                        rescale(j)

            slots(dve, slot)

        @block.gpsimd
        def _(pool):
            pool.memset(ones[:], 1.0).then_inc(ones_set, 1)
            pool.memset(ctx_nat[:, :, L:L + 1], 1.0).then_inc(ones_set, 1)
            pool.memset(ident[:], 0.0).then_inc(ident_set, 1)
            pool.wait_ge(ident_set, 1)
            pool.affine_select(out=ident[:], in_=ident[:], compare_op=ALU.not_equal, fill=1.0, base=0,
                               pattern=[[-1, P]], channel_multiplier=1).then_inc(ident_set, 1)
            pool.wait_ge(act_bounds, CTX_PARTS)
            pool.wait_ge(dve_bounds, 2)
            pool.partition_all_reduce(max_bound[:, 0:WV], own_bound[:, 0:WV], P, bass.bass_isa.ReduceOp.max)\
                .then_inc(max_bounds, 1)
            pool.wait_ge(dve_bounds, 3)
            pool.partition_all_reduce(max_bound[:, WV:], own_bound[:, WV:], P, bass.bass_isa.ReduceOp.max)\
                .then_inc(max_bounds, 1)
            for q in range(2):
                pool.sem_inc(obuf_free[q], 16)
            pool.wait_ge(constants_set, 3)
            pool.wait_ge(norm_in, 2 * 16)

            def slot(s, k, r):
                share = pool_share(s)
                if is_in(s, 0, B):
                    pool.wait_ge(v_high, s + 1)
                    pool.tensor_tensor(v_part[:, k % 2, LOW], v_scaled[:, k % 2], v_part[:, k % 2, HIGH],
                                       ALU.subtract).then_inc(v_low, 1)

                def times_gamma():
                    for j in range(share):
                        pool.wait_ge(norm_done, POOL_J * (s - 2) - moved(s) + j + 1)
                        pool.tensor_tensor(obuf[:, k % 2, j, :], obuf[:, k % 2, j, :], gamma_all[:], ALU.mult)\
                            .then_inc(pool_gamma, 1)

                def plus_beta():
                    pool.wait_ge(pool_gamma, POOL_J * (s - 2) - moved(s) + share)
                    done = pool.tensor_tensor(obuf[:, k % 2, 0:share, :], obuf[:, k % 2, 0:share, :],
                                              beta_all[:].unsqueeze(1).broadcast_to([P, share, E]), ALU.add)
                    done.then_inc(pool_out if is_in(s, 2, B) else tail_out[s - B][0], 1)

                if is_in(s, 2, B + 2):
                    times_gamma()
                if is_in(s, 2, B) or is_slot(s, B + 1):
                    plus_beta()
                if is_in(s, 1, B + 1):
                    squares = SQUARE_J if is_in(s, 1, B - 1) else RJ
                    pool.wait_ge(squares_done,
                                 SQUARE_J * s if squares < RJ else SQUARE_J * (B - 2) + RJ * (s - B + 2))
                    pool.tensor_tensor(square_mean[:, 0:squares], square_sum[:, 0:squares],
                                       one_over_e[:, 0:squares], ALU.mult).then_inc(square_mean_done, 1)
                    if squares < RJ:
                        pool.wait_ge(aggr_done, (RJ - SQUARE_J) * s)
                        pool.tensor_tensor(var_eps[:, squares:], mean_var[:, squares:, 1], eps_all[:, squares:],
                                           ALU.add)
                    pool.wait_ge(square_mean_done, s)
                    pool.tensor_tensor(var_eps[:, 0:squares], square_mean[:, 0:squares], eps_all[:, 0:squares],
                                       ALU.add).then_inc(var_ready, 1)
                    if is_slot(s, B):
                        pool.wait_ge(dve_out, s - 2)
                    elif is_in(s, 2, B):
                        pool.wait_ge(dve_out, s - 1)
                    pool.wait_ge(var_ready, s)
                    pool.tensor_tensor(rstd[:, (k + 1) % 2], var_eps[:], minus_half[:], ALU.pow)\
                        .then_inc(rstd_done, 1)
                    if squares < RJ:
                        pool.wait_ge(mean_negated, s)
                    pool.wait_ge(rstd_done, s)
                    pool.tensor_tensor(shift[:], neg_mean[:, (k + 1) % 2, 0:POOL_J], rstd[:, (k + 1) % 2, 0:POOL_J],
                                       ALU.mult).then_inc(shift_done, 1)
                if is_slot(s, B):
                    plus_beta()

            slots(pool, slot)


INPUTS = ["x", "ctx_512", "L0_xattn_Wq", "L0_xattn_bq", "L0_xattn_Wk", "L0_xattn_bk", "L0_xattn_Wv",
          "L0_xattn_bv", "L0_xattn_gamma", "L0_xattn_beta"]


def kernel(**inputs):
    import numpy as np
    import concourse.bacc as bacc
    from concourse.bass_utils import run_bass_kernel_spmd

    nc = bacc.Bacc("TRN2", target_bir_lowering=False, num_devices=1)
    arrays, args = {}, []
    for name in INPUTS:
        a = np.ascontiguousarray(inputs[name])
        arrays[f"in_{name}"] = a
        args.append(nc.dram_tensor(f"in_{name}", a.shape, mybir.dt.from_np(a.dtype), kind="ExternalInput").ap())
    out = nc.dram_tensor("out", arrays["in_x"].shape, F32, kind="ExternalOutput").ap()
    cross_attention(nc, *args, out)
    r = run_bass_kernel_spmd(nc, [arrays], core_ids=[0])
    return r.results[0]["out"]
```
